# Optimizing a Trainium2 kernel written in Bass

```python
import numpy as np
import jax
import jax.numpy as jnp

def _softmax(x, axis=-1):
    return jax.nn.softmax(x, axis=axis)

def _gelu(x):
    return jax.nn.gelu(x, approximate=True)

def _silu(x):
    return jax.nn.silu(x)

def _sigmoid(x):
    return jax.nn.sigmoid(x)

def _layernorm(x, axis=-1, eps=1e-05):
    m = jnp.mean(x, axis=axis, keepdims=True)
    v = jnp.var(x, axis=axis, keepdims=True)
    return (x - m) / jnp.sqrt(v + eps)

def _scatter_add(tgt, idx, src, axis=0):
    return tgt.at[idx].add(src)

def _segment_sum(src, seg, n):
    return jax.ops.segment_sum(src, seg, n)
kernel_name = 'mk_seq_postln_d1_jaxref_r8_047b36'

def setup_inputs(seed: int=0):
    np.random.seed(seed)
    _w = jnp.asarray

    def _L0_attn_setup():
        import jax, jax.numpy as jnp
        import numpy as np
        B, T, C = (4, 256, 128)
        NH = 16
        HS = C // NH
        key = jax.random.key(seed)
        k1, k2, k3, k4, k5 = jax.random.split(key, 5)
        s_in = 1.0 / np.sqrt(C)
        x = jax.random.normal(k1, (B, T, C), dtype=jnp.float32)
        w_attn = jax.random.normal(k2, (C, 3 * C), dtype=jnp.float32) * s_in
        b_attn = jnp.zeros((3 * C,), dtype=jnp.float32)
        w_proj = jax.random.normal(k3, (C, C), dtype=jnp.float32) * s_in
        b_proj = jnp.zeros((C,), dtype=jnp.float32)
        return {'x': x, 'w_attn': w_attn, 'b_attn': b_attn, 'w_proj': w_proj, 'b_proj': b_proj}
    _L0_attn_in = _L0_attn_setup()

    def _L0_ffn_setup():
        import jax, jax.numpy as jnp
        import numpy as np
        DIM = 128

        def _reference_tuple_inner(x, W_r, W_k, W_v, mu_r, mu_k):
            B, T, C = x.shape
            x_prev = jnp.concatenate([jnp.zeros((B, 1, C), x.dtype), x[:, :-1, :]], axis=1)
            xr = mu_r * x + (1.0 - mu_r) * x_prev
            xk = mu_k * x + (1.0 - mu_k) * x_prev
            r = jax.nn.sigmoid(jnp.einsum('btc,dc->btd', xr, W_r))
            k = jnp.einsum('btc,dc->btd', xk, W_k)
            k_act = jnp.square(jax.nn.relu(k))
            out = r * jnp.einsum('btc,dc->btd', k_act, W_v)
            new_state = x[:, -1, :]
            return (out, new_state)
        key = jax.random.key(seed)
        ks = jax.random.split(key, 6)
        B, T, C = (8, 256, DIM)
        x = jax.random.normal(ks[0], (B, T, C), dtype=jnp.float32)
        s = 1.0 / np.sqrt(C)
        W_r = jax.random.uniform(ks[1], (C, C), jnp.float32, -s, s)
        W_k = jax.random.uniform(ks[2], (C, C), jnp.float32, -s, s)
        W_v = jax.random.uniform(ks[3], (C, C), jnp.float32, -s, s)
        mu_r = jax.random.uniform(ks[4], (C,), jnp.float32)
        mu_k = jax.random.uniform(ks[5], (C,), jnp.float32)
        return {'x': x, 'W_r': W_r, 'W_k': W_k, 'W_v': W_v, 'mu_r': mu_r, 'mu_k': mu_k}
    _L0_ffn_in = _L0_ffn_setup()
    _d = {'L0_attn_x': _L0_attn_in['x'], 'L0_attn_w_attn': _L0_attn_in['w_attn'], 'L0_attn_b_attn': _L0_attn_in['b_attn'], 'L0_attn_w_proj': _L0_attn_in['w_proj'], 'L0_attn_b_proj': _L0_attn_in['b_proj'], 'L0_ffn_W_r': _L0_ffn_in['W_r'], 'L0_ffn_W_k': _L0_ffn_in['W_k'], 'L0_ffn_W_v': _L0_ffn_in['W_v'], 'L0_ffn_mu_r': _L0_ffn_in['mu_r'], 'L0_ffn_mu_k': _L0_ffn_in['mu_k']}
    _x0 = _d['L0_attn_x']
    _d['L0_attn_x'] = jax.random.normal(jax.random.fold_in(jax.random.key(seed), 1), (8, 512, 128), dtype=_x0.dtype)
    del _x0
    return _d

def reference(L0_attn_x, L0_attn_w_attn, L0_attn_b_attn, L0_attn_w_proj, L0_attn_b_proj, L0_ffn_W_r, L0_ffn_W_k, L0_ffn_W_v, L0_ffn_mu_r, L0_ffn_mu_k):

    def _L0_attn_ref(x, w_attn, b_attn, w_proj, b_proj):
        import jax, jax.numpy as jnp
        import numpy as np
        B, T, C = (4, 256, 128)
        NH = 16
        HS = C // NH
        Bsz, Tlen, Cdim = x.shape
        qkv = x @ w_attn + b_attn
        q, k, v = jnp.split(qkv, 3, axis=2)

        def heads(t):
            return t.reshape(Bsz, Tlen, NH, HS).transpose(0, 2, 1, 3)
        q, k, v = (heads(q), heads(k), heads(v))
        scale = 1.0 / np.sqrt(HS).astype(np.float32)
        att = jnp.einsum('bhqd,bhkd->bhqk', q, k) * scale
        causal = jnp.tril(jnp.ones((Tlen, Tlen), dtype=bool))
        att = jnp.where(causal, att, -jnp.inf)
        att = jax.nn.softmax(att, axis=-1)
        y = jnp.einsum('bhqk,bhkd->bhqd', att, v)
        y = y.transpose(0, 2, 1, 3).reshape(Bsz, Tlen, Cdim)
        return y @ w_proj + b_proj

    def _L0_ffn_ref(x, W_r, W_k, W_v, mu_r, mu_k):
        import jax, jax.numpy as jnp
        import numpy as np
        DIM = 128

        def _reference_tuple_inner(x, W_r, W_k, W_v, mu_r, mu_k):
            B, T, C = x.shape
            x_prev = jnp.concatenate([jnp.zeros((B, 1, C), x.dtype), x[:, :-1, :]], axis=1)
            xr = mu_r * x + (1.0 - mu_r) * x_prev
            xk = mu_k * x + (1.0 - mu_k) * x_prev
            r = jax.nn.sigmoid(jnp.einsum('btc,dc->btd', xr, W_r))
            k = jnp.einsum('btc,dc->btd', xk, W_k)
            k_act = jnp.square(jax.nn.relu(k))
            out = r * jnp.einsum('btc,dc->btd', k_act, W_v)
            new_state = x[:, -1, :]
            return (out, new_state)
        return _reference_tuple_inner(x, W_r, W_k, W_v, mu_r, mu_k)[0]
    x = L0_attn_x
    x = _layernorm(x + _L0_attn_ref(x, L0_attn_w_attn, L0_attn_b_attn, L0_attn_w_proj, L0_attn_b_proj), axis=-1)
    x = _layernorm(x + _L0_ffn_ref(x, L0_ffn_W_r, L0_ffn_W_k, L0_ffn_W_v, L0_ffn_mu_r, L0_ffn_mu_k), axis=-1)
    return x

_drawn_inputs = setup_inputs


def setup_inputs(seed=0):
    import zlib

    import numpy as np

    out = dict(_drawn_inputs(seed))
    spreads = {'L0_attn_b_attn': (0.0, 0.1), 'L0_attn_b_proj': (0.0, 0.1)}
    factors = {'L0_ffn_W_r': 3.02, 'L0_ffn_mu_r': 6.064}
    for name, (base, spread) in spreads.items():
        noise = np.random.default_rng([zlib.crc32(name.encode()), seed]).standard_normal(out[name].shape)
        drawn = base * np.exp(spread * noise) if base else spread * noise
        out[name] = jnp.asarray(drawn.astype(out[name].dtype))
    for name, factor in factors.items():
        out[name] = (out[name] * factor).astype(out[name].dtype)
    return out
```

```python
from contextlib import ExitStack

import concourse.bass as bass
from concourse import mybir

F32 = mybir.dt.float32
BF16 = mybir.dt.bfloat16
U32 = mybir.dt.uint32
ALU = mybir.AluOpType
ACT = mybir.ActivationFunctionType
AX_X = mybir.AxisListType.X

P = 128
NB, T, C = 8, 512, 128
NH = 16
HD = C // NH
NT = T // P
HG = 4
SLOTS = NH // HG
SCALE = float(HD) ** -0.5
EPS = 1e-5
MASKED = -1e30

Q_PARTS = (0, 0, 0, 1, 1, 2)
K_PARTS = (0, 1, 2, 0, 1, 0)
MAX_ROW = len(Q_PARTS) * HD

VW = 32
PCOL = (0, 512, 1024, 896)
PW = 1280

EX_UNITS = 10
MX_UNITS = 12
MX_BANKS = 3
EX_BANKS = 2

SHARED_ORDER = (
    "maxT0 Y0 xT q k v "
    "maxT1 Y1 ynT proj "
    "maxT2 Y2 x1T "
    "maxT3 Y3 kT r kv"
).split()
HEAD_ORDER = "xT q k v wT bp maxT3".split()
TAIL_ORDER = "Y0 Y1 ynT proj x1T kT r kv".split()
SHARED_BANK = dict.fromkeys("maxT0 maxT1 maxT2 maxT3 xT k ynT x1T kT wT".split(), 0) | \
    dict.fromkeys("Y0 Y1 Y2 Y3 q v proj r kv bp".split(), 1)


def shared_uses():
    n, at = [0, 0], {}
    for name in HEAD_ORDER:
        n[SHARED_BANK[name]] += 1
        at[-1, name] = n[SHARED_BANK[name]]
    for b in range(NB):
        for name in SHARED_ORDER:
            prev_missing = b == 0 and name in ("Y0", "Y1", "ynT", "proj", "x1T", "kT", "r", "kv")
            next_missing = b == NB - 1 and name in ("xT", "q", "k", "v", "maxT3")
            if not (prev_missing or next_missing):
                n[SHARED_BANK[name]] += 1
                at[b, name] = n[SHARED_BANK[name]]
    for name in TAIL_ORDER:
        n[SHARED_BANK[name]] += 1
        at[NB, name] = n[SHARED_BANK[name]]
    return at


SHARED_USES = shared_uses()
LOOP_FROM, LOOP_TO = 2, 6


def shared_use(name, b):
    if isinstance(b, int):
        return SHARED_USES[b, name]
    first = SHARED_USES[LOOP_FROM, name]
    per = SHARED_USES[LOOP_FROM + 1, name] - first
    return (b - LOOP_FROM) * per + first


def wait(eng, sem, value):
    if not isinstance(value, int) or value > 0:
        eng.wait_ge(sem, value)


def wait_apart(eng, sem, value, passed):
    wait(eng, sem, value)
    if not isinstance(value, int):
        eng.sem_inc(passed, 1)


def block_kernel(nc, x, w_attn, b_attn, w_proj, b_proj, W_r, W_k, W_v, mu_r, mu_k, out):
    with ExitStack() as ctx:
        def sb(name, shape, dt=F32):
            return ctx.enter_context(nc.sbuf_tensor(name, shape, dt))

        def sem(name):
            return ctx.enter_context(nc.semaphore(name))

        ident = sb("ident", [P, P])
        ident_b = sb("ident_b", [P, P], BF16)
        mask_b = sb("mask_b", [P, P], BF16)
        neg_one = sb("neg_one", [2 * NH, T], BF16)
        zero_b = sb("zero_b", [2 * NH, T], BF16)
        w_in = sb("w_in", [P, 3 * C])
        w_q = sb("w_q", [P, C])
        w_k = sb("w_k", [P, C])
        w_o = sb("w_o", [P, C])
        w_ffn = sb("w_ffn", [P, 3, C])
        w_ffnT = sb("w_ffnT", [P, 3, C])
        b_q = sb("b_q", [P, 1])
        b_k = sb("b_k", [P, 1])
        b_v = sb("b_v", [P, 1])
        b_v_wide = sb("b_v_wide", [P, P])
        b_o = sb("b_o", [P, C])
        b_out = sb("b_out", [P, C])
        mu = [sb(f"mu{i}", [P, 1]) for i in range(2)]
        mu_rest = [sb(f"mu_rest{i}", [P, 1]) for i in range(2)]
        exponent = sb("exponent", [P, NT])

        x_in = [sb(f"x_in{i}", [P, NT, C]) for i in range(2)]
        x_res = [sb(f"x_res{i}", [P, NT, C]) for i in range(2)]
        xT = sb("xT", [P, T])
        q_part = sb("q_part", [P, 3, T], BF16)
        k_part = sb("k_part", [P, 3, T], BF16)
        q_rest = sb("q_rest", [P, T])
        k_rest = sb("k_rest", [P, T])
        q_st = [sb(f"q_st{i}", [P, NH, T], BF16) for i in range(2)]
        k_st = [sb(f"k_st{i}", [P, NH, T], BF16) for i in range(2)]
        vals = [sb(f"vals{i}", [P, NT, NH, VW]) for i in range(2)]
        yn = sb("yn", [P, NT, C])
        ynT = sb("ynT", [P, T])
        h1 = sb("h1", [P, NT, C])
        x1 = sb("x1", [P, NT, C])
        mix_cur = [sb(f"mix_cur{i}", [P, T]) for i in range(2)]
        mix_prev = [sb(f"mix_prev{i}", [P, T]) for i in range(2)]
        mixT = [sb(f"mixT{i}", [P, T]) for i in range(2)]
        gate = sb("gate", [P, NT, C])
        relu = sb("relu", [P, T])
        kact = sb("kact", [P, T])
        gated = sb("gated", [P, NT, C])
        h2 = sb("h2", [P, NT, C])
        o_sb = sb("o_sb", [P, NT, C])
        stats = [sb(f"stats{i}", [P, NT, 6]) for i in range(2)]
        mv = [sb(f"mv{i}", [P, NT, 2]) for i in range(2)]
        var_eps = [sb(f"var_eps{i}", [P, NT]) for i in range(2)]
        rstd = [sb(f"rstd{i}", [P, NT]) for i in range(2)]

        m_max = [sb(f"m_max{i}", [P, NT, HG]) for i in range(2)]
        m_part = sb("m_part", [P, NT, 2, HG], BF16)
        m_rows = sb("m_rows", [2 * HG, T], BF16)
        probs = [sb(f"probs{i}", [P, HG, PW]) for i in range(2)]
        yT = sb("yT", [P, T])
        rden = sb("rden", [P, NT, HG])

        def bank_of(name):
            return ctx.enter_context(nc.psum_tensor(name, [P, T], F32))

        mx_ps = [bank_of(f"mx_ps{i}") for i in range(MX_BANKS)]
        ex_ps = [bank_of(f"ex_ps{i}") for i in range(EX_BANKS)]
        pv_ps = bank_of("pv_ps")
        sh_ps = [bank_of(f"sh_ps{i}") for i in range(2)]

        w_in_loaded, w_loaded = sem("w_in_loaded"), sem("w_loaded")
        b_qk_loaded, vecs_loaded = sem("b_qk_loaded"), sem("vecs_loaded")
        xin_loaded = [sem(f"xin_loaded{i}") for i in range(2)]
        xres_loaded = [sem(f"xres_loaded{i}") for i in range(2)]
        consts_g = sem("consts_g")
        consts_v = sem("consts_v")
        ones_stacked = [sem(f"ones_stacked{i}") for i in range(2)]
        q_stacked, k_stacked = sem("q_stacked"), sem("k_stacked")
        rows_stacked = sem("rows_stacked")
        mx_full, mx_read = sem("mx_full"), sem("mx_read")
        ex_full, exp_done = sem("ex_full"), sem("exp_done")
        m_hi, m_parts = sem("m_hi"), sem("m_parts")
        causal = sem("causal")
        pv_done, yT_done, rden_done = sem("pv_done"), sem("yT_done"), sem("rden_done")
        sh_full = [sem(f"sh_full{i}") for i in range(2)]
        sh_read = [sem(f"sh_read{i}") for i in range(2)]
        high = [sem("q_high"), sem("k_high")]
        mid = [sem("q_mid"), sem("k_mid")]
        low = [sem("q_low"), sem("k_low")]
        xres_ready = sem("xres_ready")
        bn = [sem("bn1"), sem("bn2")]
        mean_var = [sem("mean_var1"), sem("mean_var2")]
        var_ready = [sem("var_ready1"), sem("var_ready2")]
        rstd_ready = [sem("rstd_ready1"), sem("rstd_ready2")]
        x1_done, o_done, h2_done = sem("x1_done"), sem("o_done"), sem("h2_done")
        mixed = sem("mixed")
        kact_done = sem("kact_done")
        stored = sem("stored")
        passed_v, passed_g, passed_s = sem("passed_v"), sem("passed_g"), sem("passed_s")

        x_d = x.rearrange("b (t p) c -> b p t c", p=P)
        out_d = out.rearrange("b (t p) c -> b p t c", p=P)
        Q_DMAS = 16 * (len(Q_PARTS) + 1)
        K_DMAS = 16 * len(K_PARTS)

        def fixed(b):
            return isinstance(b, int)

        def has_prev(b):
            return not fixed(b) or b >= 1

        def has_next(b):
            return not fixed(b) or b <= NB - 2

        def exists(b, g):
            return not fixed(b) or 0 <= SLOTS * b + g < NB * SLOTS

        def over_sequences(eng, body):
            for b in range(LOOP_FROM):
                body(b, b % 2)
            with eng.Fori(LOOP_FROM // 2, LOOP_TO // 2) as i:
                for par in range(2):
                    body(i * 2 + par, par)
            for b in range(LOOP_TO, NB):
                body(b, b % 2)

        def wait_full(eng, name, b):
            i = SHARED_BANK[name]
            wait(eng, sh_full[i], shared_use(name, b))
            return sh_ps[i], sh_read[i]

        def wait_read(eng, name, b):
            wait(eng, sh_read[SHARED_BANK[name]], shared_use(name, b))

        block = ctx.enter_context(nc.Block())

        @block.sync
        def _(sp):
            def stack(which, b, par):
                wait_apart(sp, exp_done, (b - 1) * (SLOTS * EX_UNITS), passed_s)
                wait(sp, low[which], b + 1)
                st, part_of, sem_of = ((q_st[par], q_part, q_stacked), (k_st[par], k_part, k_stacked))[which]
                if which == 0:
                    sp.dma_start(st[MAX_ROW:MAX_ROW + 2, :, :], zero_b[:, :]).then_inc(q_stacked, 16)
                for band, part in enumerate((Q_PARTS, K_PARTS)[which]):
                    sp.dma_start(st[band * HD:(band + 1) * HD, :, :], part_of[:, part, :]).then_inc(sem_of, 16)

            def stack_maxima(b, par, g, step_b, name):
                wait_read(sp, name, step_b)
                sp.dma_start(q_st[par][MAX_ROW:MAX_ROW + 2, g * HG:(g + 1) * HG, :],
                             m_rows[:, :]).then_inc(rows_stacked, 16)

            def store(b):
                wait(sp, o_done, b * NT + NT)
                sp.dma_start(out_d[b], o_sb[:, :, :]).then_inc(stored, 16)

            sp.dma_start(x_in[0][:, :, :], x_d[0]).then_inc(xin_loaded[0], 16)
            sp.dma_start(w_in[:, :], w_attn).then_inc(w_in_loaded, 16)
            sp.dma_start(b_q[:, :], b_attn[0:C].rearrange("(h d a) -> d h a", d=HD, a=1),
                         allow_slow_non_contiguous=True).then_inc(b_qk_loaded, 16)
            sp.dma_start(b_k[:, :], b_attn[C:2 * C].rearrange("(h d a) -> d h a", d=HD, a=1),
                         allow_slow_non_contiguous=True).then_inc(b_qk_loaded, 16)
            for w, wd in enumerate((W_r, W_k, W_v)):
                sp.dma_start(w_ffn[:, w, :], wd).then_inc(w_loaded, 16)
            sp.dma_start(w_o[:, :], w_proj).then_inc(w_loaded, 16)
            sp.dma_start(b_v[:, :], b_attn[2 * C:3 * C].rearrange("(p a) -> p a", a=1)).then_inc(vecs_loaded, 16)
            sp.dma_start(b_o[:, :], b_proj.partition_broadcast(P)).then_inc(vecs_loaded, 16)
            for i, m in enumerate((mu_r, mu_k)):
                sp.dma_start(mu[i][:, :], m.rearrange("(p a) -> p a", a=1)).then_inc(vecs_loaded, 16)
            sp.wait_ge(consts_g, 5)
            sp.dma_start(k_st[0][MAX_ROW:MAX_ROW + 2, :, :], neg_one[:, :]).then_inc(ones_stacked[0], 16)
            sp.wait_ge(consts_v, 1)
            stack(0, 0, 0)
            stack(1, 0, 0)
            sp.dma_start(x_in[1][:, :, :], x_d[1]).then_inc(xin_loaded[1], 16)
            sp.wait_ge(consts_g, 12)
            sp.dma_start(k_st[1][MAX_ROW:MAX_ROW + 2, :, :], neg_one[:, :]).then_inc(ones_stacked[1], 16)
            sp.wait_ge(consts_v, 7)
            stack_maxima(0, 0, 0, -1, "maxT3")

            def body(b, par):
                for g in range(SLOTS):
                    if g == 0:
                        if not fixed(b) or b >= 2:
                            wait_read(sp, "proj", b - 1)
                        sp.dma_start(x_res[par][:, :, :], x_d[b]).then_inc(xres_loaded[par], 16)
                    if exists(b, g + 1):
                        if g < SLOTS - 1:
                            stack_maxima(b, par, g + 1, b, f"maxT{g}")
                        else:
                            stack_maxima(b + 1, 1 - par, 0, b, f"maxT{g}")
                    if g < 2 and has_next(b):
                        stack(g, b + 1, 1 - par)
                    if g == 2 and (not fixed(b) or b >= 2):
                        store(b - 2)
                    if g == 3 and (not fixed(b) or b + 2 < NB):
                        wait_read(sp, "xT", b - 1)
                        sp.dma_start(x_in[par][:, :, :], x_d[b + 2]).then_inc(xin_loaded[par], 16)

            over_sequences(sp, body)
            store(NB - 2)
            store(NB - 1)
            sp.wait_ge(stored, 16 * NB)

        @block.tensor
        def _(pe):
            mm = pe.matmul

            def bank(name, b):
                i = SHARED_BANK[name]
                wait(pe, sh_read[i], shared_use(name, b) - 1)
                return sh_ps[i], sh_full[i]

            def transpose4(name, b, src):
                ps, full = bank(name, b)
                for t in range(NT):
                    last = pe.transpose(ps[:, t * P:(t + 1) * P], src(t), ident[:, :])
                last.then_inc(full, 1)

            def product4(name, b, lhs, rhs):
                ps, full = bank(name, b)
                for t in range(NT):
                    last = mm(ps[:, t * P:(t + 1) * P], lhs[:, t * P:(t + 1) * P], rhs, start=True, stop=True)
                last.then_inc(full, 1)

            def product(name, b, lhs, rhs):
                ps, full = bank(name, b)
                mm(ps[:, :], lhs, rhs, start=True, stop=True).then_inc(full, 1)

            def x_transposed(step_b, b, par):
                wait(pe, xin_loaded[par], (b // 2 + 1) * 16 if fixed(b) else (b - par) * 8 + 16)
                transpose4("xT", step_b, lambda t: x_in[par][:, t, :])

            def queries_keys(step_b):
                wait_read(pe, "xT", step_b)
                product("q", step_b, w_q[:, :], xT[:, :])
                product("k", step_b, w_k[:, :], xT[:, :])

            def values(step_b):
                product4("v", step_b, xT, w_in[:, 2 * C:3 * C])

            def maxima(b, par, g, hh):
                if g == 0 and hh == 0:
                    wait(pe, q_stacked, b * Q_DMAS + Q_DMAS)
                    wait(pe, k_stacked, b * K_DMAS + K_DMAS)
                u0 = 6 * (hh // 2) + 2 * (hh % 2)
                units = [[(hh, 3)], [(hh, 2)]]
                if hh % 2:
                    units += [[(hh - 1, 1), (hh, 1)], [(hh - 1, 0), (hh, 0)]]
                for u, parts in enumerate(units, u0):
                    wait(pe, mx_read, b * (SLOTS * MX_UNITS) + (g * MX_UNITS + u - MX_BANKS + 1))
                    ps, at = mx_ps[u % MX_BANKS], 0
                    for h, t in parts:
                        n, hd = (t + 1) * P, g * HG + h
                        mm(ps[:, at:at + n], q_st[par][:, hd, t * P:(t + 1) * P], k_st[par][:, hd, 0:n],
                           start=True, stop=False, skip_group_check=True)
                        at += n
                        last = mm(ps[:, at - P:at], ident_b[:, :], mask_b[:, :],
                                  start=False, stop=True, skip_group_check=True)
                    last.then_inc(mx_full, 1)

            def logits(b, par, g, hh):
                if hh == 0:
                    wait(pe, rows_stacked, b * (SLOTS * 16) + (g * 16 + 16))
                units = [[(hh, 0)], [(hh, 1), (hh, 3)]]
                if hh % 2:
                    units.append([(hh - 1, 2), (hh, 2)])
                for u, parts in enumerate(units, 5 * (hh // 2) + 2 * (hh % 2)):
                    wait(pe, exp_done, b * (SLOTS * EX_UNITS) + (g * EX_UNITS + u - EX_BANKS + 1))
                    ps, at = ex_ps[u % EX_BANKS], 0
                    for h, t in parts:
                        n, hd = T - t * P, g * HG + h
                        last = mm(ps[:, at:at + n], k_st[par][:, hd, t * P:(t + 1) * P], q_st[par][:, hd, t * P:T],
                                  start=True, stop=True)
                        at += n
                    last.then_inc(ex_full, 1)

            def max_transposed(name, step_b, b, g):
                wait(pe, m_parts, b * SLOTS + (g + 1))
                ps, full = bank(name, step_b)
                for t in range(NT):
                    last = mm(ps[0:2 * HG, t * P:(t + 1) * P], m_part[:, t, :, :], ident_b[:, :],
                              start=True, stop=True)
                last.then_inc(full, 1)

            def weighted_values(b, par, g, t):
                if t == 0:
                    wait(pe, causal, b * (SLOTS * 2 * NT) + (g + 1) * (2 * NT))
                    wait(pe, yT_done, b * SLOTS + g)
                if g == 0 and t == 0:
                    wait_read(pe, "v", b - 1)
                for h in range(HG):
                    last = mm(pv_ps[h * VW:(h + 1) * VW, t * P:T], vals[par][:, t, g * HG + h, :],
                              probs[g % 2][:, h, PCOL[t]:PCOL[t] + T - t * P],
                              start=(t == 0), stop=(t == NT - 1), skip_group_check=True)
                if t == NT - 1:
                    last.then_inc(pv_done, 1)

            def back_to_rows(name, step_b, b, g):
                wait(pe, yT_done, b * SLOTS + (g + 1))
                transpose4(name, step_b, lambda t: yT[:, t * P:(t + 1) * P])

            def attention_transposed(step_b):
                wait_read(pe, "Y1", step_b)
                transpose4("ynT", step_b, lambda t: yn[:, t, :])

            def project(step_b):
                wait_read(pe, "ynT", step_b)
                product4("proj", step_b, ynT, w_o[:, :])

            def x1_transposed(step_b, b):
                wait(pe, x1_done, b * NT + NT)
                transpose4("x1T", step_b, lambda t: x1[:, t, :])

            def ffn_in(step_b, b):
                wait(pe, mixed, b * 2 + 2)
                product("kT", step_b, w_ffnT[:, 1, :], mixT[1][:, :])
                product4("r", step_b, mixT[0], w_ffnT[:, 0, :])

            def ffn_out(step_b, b):
                wait(pe, kact_done, b + 1)
                product4("kv", step_b, kact, w_ffnT[:, 2, :])

            pe.wait_ge(consts_g, 2)
            x_transposed(-1, 0, 0)
            pe.wait_ge(consts_v, 3)
            queries_keys(-1)
            values(-1)
            pe.wait_ge(w_loaded, 64)
            ps, full = bank("wT", -1)
            for w in range(3):
                last = pe.transpose(ps[:, w * P:(w + 1) * P], w_ffn[:, w, :], ident[:, :])
            last.then_inc(full, 1)
            pe.wait_ge(consts_v, 4)
            ps, full = bank("bp", -1)
            mm(ps[:, 0:C], b_v_wide[:, :], w_o[:, :], start=True, stop=True).then_inc(full, 1)
            pe.wait_ge(consts_g, 9)
            pe.wait_ge(ones_stacked[0], 16)
            for hh in range(HG):
                maxima(0, 0, 0, hh)
            for hh in range(HG):
                maxima(0, 0, 1, hh)
                if hh == 0:
                    max_transposed("maxT3", -1, 0, 0)
            pe.wait_ge(ones_stacked[1], 16)

            def body(b, par):
                for g in range(SLOTS):
                    for hh in range(HG):
                        logits(b, par, g, hh)
                        if hh == 0 and exists(b, g + 1):
                            max_transposed(f"maxT{g}", b, b, g + 1)
                        if exists(b, g + 2):
                            if g < 2:
                                maxima(b, par, g + 2, hh)
                            else:
                                maxima(b + 1, 1 - par, g - 2, hh)
                        if exists(b, g - 1):
                            if g:
                                weighted_values(b, par, g - 1, hh)
                            else:
                                weighted_values(b - 1, 1 - par, SLOTS - 1, hh)
                        if hh == 1 and exists(b, g - 2):
                            back_to_rows(f"Y{g}", b, b, g - 2)
                        if g == 0 and has_next(b):
                            if hh == 1:
                                x_transposed(b, b + 1, 1 - par)
                            elif hh == 2:
                                queries_keys(b)
                            elif hh == 3:
                                values(b)
                        if has_prev(b):
                            if (g, hh) == (1, 2):
                                attention_transposed(b)
                            elif (g, hh) == (1, 3):
                                project(b)
                            elif (g, hh) == (2, 2):
                                x1_transposed(b, b - 1)
                            elif (g, hh) == (3, 2):
                                ffn_in(b, b - 1)
                            elif (g, hh) == (3, 3):
                                ffn_out(b, b - 1)

            over_sequences(pe, body)

            last_b = NB - 1
            back_to_rows("Y0", NB, last_b, SLOTS - 2)
            for t in range(NT):
                weighted_values(last_b, last_b % 2, SLOTS - 1, t)
            back_to_rows("Y1", NB, last_b, SLOTS - 1)
            attention_transposed(NB)
            project(NB)
            x1_transposed(NB, last_b)
            ffn_in(NB, last_b)
            ffn_out(NB, last_b)

        @block.scalar
        def _(act):
            def copy(name, b, dst, cols=T):
                ps, read = wait_full(act, name, b)
                act.activation(dst, ps[0:dst.shape[0], 0:cols], ACT.Copy).then_inc(read, 1)

            def exps(b, g, hh):
                if hh == 0:
                    wait(act, pv_done, b * SLOTS + (g - 1))
                pr = probs[g % 2]
                to = [pr[:, hh, 0:T], pr[:, hh, T:2 * T]]
                if hh % 2:
                    to.append(pr[:, hh - 1:hh + 1, 2 * T:PW])
                for u, dst in enumerate(to, 5 * (hh // 2) + 2 * (hh % 2)):
                    wait(act, ex_full, b * (SLOTS * EX_UNITS) + (g * EX_UNITS + u + 1))
                    src = ex_ps[u % EX_BANKS][:, :]
                    if u % 5 == 4:
                        src = src.rearrange("p (h q) -> p h q", h=2)
                    act.activation(dst, src, ACT.Exp, scale=SCALE).then_inc(exp_done, 1)

            def max_rows(name, step_b, n):
                wait(act, rows_stacked, n * 16)
                copy(name, step_b, m_rows[:, :])

            def sums(b, g):
                wait(act, pv_done, b * SLOTS + (g + 1))
                act.activation(yT[:, :], pv_ps[:, :], ACT.Copy).then_inc(yT_done, 1)

            def highs(step_b, b):
                for i, (name, part, bias) in enumerate((("q", q_part, b_q), ("k", k_part, b_k))):
                    wait(act, (q_stacked, k_stacked)[i], b * (Q_DMAS, K_DMAS)[i])
                    ps, _ = wait_full(act, name, step_b)
                    act.activation(part[:, 0, :], ps[:, :], ACT.Identity, bias=bias[:, 0:1]).then_inc(high[i], 1)

            def mids(step_b, b):
                for i, (name, part, rest) in enumerate((("q", q_part, q_rest), ("k", k_part, k_rest))):
                    wait_read(act, name, step_b)
                    act.activation(part[:, 1, :], rest[:, :], ACT.Copy).then_inc(mid[i], 1)

            def values(step_b, b, par):
                wait(act, pv_done, b * SLOTS - SLOTS)
                ps, read = wait_full(act, "v", step_b)
                act.activation(vals[par][:, :, :, 0:HD], ps[:, :].rearrange("p (t h d) -> p t h d", t=NT, h=NH),
                               ACT.Copy).then_inc(read, 1)

            def shares(step_b, b):
                wait(act, mixed, b * 2)
                ps, read = wait_full(act, "x1T", step_b)
                for i in range(2):
                    act.activation(mix_cur[i][:, :], ps[:, :], ACT.Copy, scale=mu[i][:, 0:1])
                for i in range(2):
                    last = act.activation(mix_prev[i][:, 1:T], ps[:, 0:T - 1], ACT.Copy, scale=mu_rest[i][:, 0:1])
                last.then_inc(read, 1)

            def ffn_nonlinear(step_b):
                ps, read = wait_full(act, "kT", step_b)
                act.activation(relu[:, :], ps[:, :], ACT.Relu).then_inc(read, 1)
                ps, read = wait_full(act, "r", step_b)
                act.activation(gate[:, :, :], ps[:, :].rearrange("p (t c) -> p t c", t=NT), ACT.Tanh, scale=0.5
                               ).then_inc(read, 1)

            copy("xT", -1, xT[:, :])
            act.wait_ge(b_qk_loaded, 32)
            highs(-1, 0)
            mids(-1, 0)
            act.wait_ge(consts_g, 11)
            values(-1, 0, 0)
            copy("wT", -1, w_ffnT[:, :, :].rearrange("p w c -> p (w c)"), 3 * C)
            max_rows("maxT3", -1, 0)
            act.wait_ge(consts_g, 14)
            act.wait_ge(consts_v, 6)

            def body(b, par):
                for g in range(SLOTS):
                    for hh in range(HG):
                        exps(b, g, hh)
                        if hh == 0:
                            if exists(b, g - 2):
                                if exists(b, g - 3):
                                    if g:
                                        wait_read(act, f"Y{g - 1}", b)
                                    else:
                                        wait_read(act, "Y3", b - 1)
                                sums(b, g - 2)
                            if exists(b, g + 1):
                                max_rows(f"maxT{g}", b, b * SLOTS + (g + 1))
                        if g == 0 and has_next(b):
                            if hh == 1:
                                copy("xT", b, xT[:, :])
                            elif hh == 2:
                                highs(b, b + 1)
                            elif hh == 3:
                                mids(b, b + 1)
                                values(b, b + 1, 1 - par)
                        if has_prev(b):
                            if (g, hh) == (1, 2):
                                copy("ynT", b, ynT[:, :])
                            elif (g, hh) == (2, 2):
                                shares(b, b - 1)
                            elif (g, hh) == (3, 2):
                                ffn_nonlinear(b)

            over_sequences(act, body)

            last_b = NB - 1
            wait_read(act, "Y3", last_b)
            sums(last_b, SLOTS - 2)
            wait_read(act, "Y0", NB)
            sums(last_b, SLOTS - 1)
            copy("ynT", NB, ynT[:, :])
            shares(NB, last_b)
            ffn_nonlinear(NB)

        @block.vector
        def _(dve):
            def reduce_maxima(b, g, hh):
                m = m_max[g % 2]
                to = [(m[:, 3, hh:hh + 1], 4 * P, 1), (m[:, 2, hh:hh + 1], 3 * P, 1)]
                if hh % 2:
                    to += [(m[:, t, hh - 1:hh + 1], (t + 1) * P, 2) for t in (1, 0)]
                for u, (dst, n, heads) in enumerate(to, 6 * (hh // 2) + 2 * (hh % 2)):
                    wait(dve, mx_full, b * (SLOTS * MX_UNITS) + (g * MX_UNITS + u + 1))
                    src = mx_ps[u % MX_BANKS][:, 0:n * heads].rearrange("p (h k) -> p h k", h=heads)
                    dve.tensor_reduce(dst, src, AX_X, ALU.max).then_inc(mx_read, 1)

            def max_parts(b, g, before, before_b):
                s, m = b * SLOTS + g, m_max[g % 2]
                wait(dve, mx_read, b * (SLOTS * MX_UNITS) + (g + 1) * MX_UNITS)
                if before:
                    wait_full(dve, before, before_b)
                dve.tensor_copy(m_part[:, :, 0, :], m[:, :, :]).then_inc(m_hi, 1)
                wait(dve, m_hi, s + 1)
                dve.tensor_tensor(m_part[:, :, 1, :], m[:, :, :], m_part[:, :, 0, :], ALU.subtract).then_inc(m_parts, 1)

            def rests(step_b, b):
                for i, (name, part, rest, bias) in enumerate((("q", q_part, q_rest, b_q), ("k", k_part, k_rest, b_k))):
                    wait(dve, high[i], b + 1)
                    wait(dve, low[i], b)
                    ps, read = wait_full(dve, name, step_b)
                    dve.scalar_tensor_tensor(out=rest[:, :], in0=ps[:, :], scalar=bias[:, 0:1], in1=part[:, 0, :],
                                             op0=ALU.add, op1=ALU.subtract).then_inc(read, 1)

            def normalise(name, step_b, b, g):
                ps, read = wait_full(dve, name, step_b)
                y = ps[:, :].rearrange("p (t h w) -> p t h w", t=NT, h=HG)
                dve.reciprocal(rden[:, :, :], y[:, :, :, HD]).then_inc(rden_done, 1)
                wait(dve, rden_done, b * SLOTS + (g + 1))
                if g == 0 and has_prev(b):
                    wait_full(dve, "ynT", step_b)
                dst = yn[:, :, g * HG * HD:(g + 1) * HG * HD].rearrange("p t (h d) -> p t h d", h=HG)
                dve.tensor_tensor(dst, y[:, :, :, 0:HD], rden[:, :, :].unsqueeze(3).to_broadcast([P, NT, HG, HD]),
                                  ALU.mult).then_inc(read, 1)

            def statistics(i, b, src):
                wait(dve, rstd_ready[i], b)
                for t in range(NT):
                    dve.bn_stats(stats[i][:, t, :], src[:, t, :]).then_inc(bn[i], 1)
                wait_apart(dve, bn[i], b * NT + NT, passed_v)
                for t in range(NT):
                    dve.bn_aggr(mv[i][:, t, :], stats[i][:, t, :]).then_inc(mean_var[i], 1)

            def normed(i, b, src, dst, done):
                wait(dve, rstd_ready[i], b + 1)
                for t in range(NT):
                    dve.tensor_scalar(dst[:, t, :], src[:, t, :], mv[i][:, t, 0:1], rstd[i][:, t:t + 1],
                                      ALU.subtract, ALU.mult).then_inc(done, 1)

            def attention_added(step_b, b, par):
                wait(dve, xres_ready, b + 1)
                wait(dve, x1_done, b * NT)
                ps, read = wait_full(dve, "proj", step_b)
                dve.tensor_tensor(h1[:, :, :], ps[:, :].rearrange("p (t c) -> p t c", t=NT), x_res[par][:, :, :],
                                  ALU.add).then_inc(read, 1)
                wait_read(dve, "proj", step_b)
                statistics(0, b, h1)

            def attention_normed(step_b, b):
                wait(dve, h2_done, b)
                normed(0, b, h1, x1, x1_done)

            def ffn_added(step_b, b):
                wait(dve, o_done, b * NT)
                ps, read = wait_full(dve, "kv", step_b)
                wait_read(dve, "r", step_b)
                dve.scalar_tensor_tensor(out=gated[:, :, :], in0=gate[:, :, :], scalar=1.0,
                                         in1=ps[:, :].rearrange("p (t c) -> p t c", t=NT),
                                         op0=ALU.add, op1=ALU.mult).then_inc(read, 1)
                wait_read(dve, "kv", step_b)
                dve.scalar_tensor_tensor(out=h2[:, :, :], in0=gated[:, :, :], scalar=0.5, in1=x1[:, :, :],
                                         op0=ALU.mult, op1=ALU.add).then_inc(h2_done, 1)
                wait(dve, h2_done, b + 1)
                statistics(1, b, h2)

            def ffn_normed(b):
                wait(dve, stored, b * 16)
                normed(1, b, h2, o_sb, o_done)

            dve.memset(q_st[0][:, :, :].bitcast(U32), 0).then_inc(consts_v, 1)
            dve.wait_ge(w_in_loaded, 16)
            for i, w in enumerate((w_q, w_k)):
                dve.tensor_copy(w[:, :].rearrange("p (d h) -> p d h", d=HD),
                                w_in[:, i * C:(i + 1) * C].rearrange("p (h d) -> p d h", d=HD)).then_inc(consts_v, 1)
            dve.wait_ge(vecs_loaded, 64)
            dve.tensor_copy(b_v_wide[:, :], b_v[:, 0:1].to_broadcast([P, P])).then_inc(consts_v, 1)
            for i in range(2):
                dve.tensor_scalar(mu_rest[i][:, :], mu[i][:, :], -1.0, 1.0, ALU.mult, ALU.add).then_inc(consts_v, 1)
            dve.wait_ge(b_qk_loaded, 32)
            rests(-1, 0)
            dve.memset(q_st[1][:, :, :].bitcast(U32), 0).then_inc(consts_v, 1)
            ps, read = wait_full(dve, "bp", -1)
            dve.tensor_tensor(b_out[:, :], ps[:, 0:C], b_o[:, :], ALU.add).then_inc(read, 1)
            for g in range(2):
                for hh in range(HG):
                    reduce_maxima(0, g, hh)
                max_parts(0, g, "maxT3" if g else None, -1)

            def body(b, par):
                for g in range(SLOTS):
                    for hh in range(HG):
                        if exists(b, g + 2):
                            if g < 2:
                                reduce_maxima(b, g + 2, hh)
                            else:
                                reduce_maxima(b + 1, g - 2, hh)
                        if hh == 1 and exists(b, g - 2):
                            if g < 2:
                                normalise(f"Y{g}", b, b - 1, g + 2)
                            else:
                                normalise(f"Y{g}", b, b, g - 2)
                        if (g, hh) == (0, 2) and has_next(b):
                            rests(b, b + 1)
                        if not fixed(b) or b >= 2:
                            if (g, hh) == (0, 0):
                                ffn_added(b - 1, b - 2)
                            elif (g, hh) == (0, 1):
                                ffn_normed(b - 2)
                        if has_prev(b):
                            if (g, hh) == (2, 0):
                                attention_added(b, b - 1, 1 - par)
                            elif (g, hh) == (2, 1):
                                attention_normed(b, b - 1)
                    if exists(b, g + 2):
                        if g < 2:
                            max_parts(b, g + 2, f"maxT{g}", b)
                        else:
                            max_parts(b + 1, g - 2, f"maxT{g}", b)

            over_sequences(dve, body)

            last_b = NB - 1
            ffn_added(last_b, last_b - 1)
            ffn_normed(last_b - 1)
            normalise("Y0", NB, last_b, SLOTS - 2)
            normalise("Y1", NB, last_b, SLOTS - 1)
            attention_added(NB, last_b, last_b % 2)
            attention_normed(NB, last_b)
            ffn_added(NB, last_b)
            ffn_normed(last_b)

        @block.gpsimd
        def _(pool):
            def zero_behind(b, g, pair):
                wait_apart(pool, exp_done, b * (SLOTS * EX_UNITS) + (g * EX_UNITS + 5 * pair + 5), passed_g)
                for t in range(NT):
                    blocks = probs[g % 2][:, 2 * pair:2 * pair + 2, PCOL[t]:PCOL[t] + P]
                    pool.affine_select(out=blocks, in_=blocks, compare_op=ALU.is_ge, fill=0.0, base=0,
                                       pattern=[[0, 2], [1, P]], channel_multiplier=-1).then_inc(causal, 1)

            def lows(b):
                for i, (part, rest) in enumerate(((q_part, q_rest), (k_part, k_rest))):
                    wait(pool, mid[i], b + 1)
                    pool.tensor_tensor(part[:, 2, :], rest[:, :], part[:, 1, :], ALU.subtract).then_inc(low[i], 1)

            def residual_biased(b, par):
                wait(pool, xres_loaded[par], (b // 2 + 1) * 16 if fixed(b) else (b - par) * 8 + 16)
                pool.tensor_tensor(x_res[par][:, :, :], x_res[par][:, :, :],
                                   b_out[:, :].unsqueeze(1).to_broadcast([P, NT, C]), ALU.add).then_inc(xres_ready, 1)

            def deviations(i, b):
                wait(pool, mean_var[i], b * NT + NT)
                wait_apart(pool, (x1_done, o_done)[i], b * NT, passed_g)
                pool.tensor_scalar(var_eps[i][:, :], mv[i][:, :, 1], EPS, None, ALU.add).then_inc(var_ready[i], 1)
                wait(pool, var_ready[i], b + 1)
                pool.tensor_tensor(rstd[i][:, :], var_eps[i][:, :], exponent[:, :], ALU.pow).then_inc(rstd_ready[i], 1)

            def mix(step_b, b):
                wait_read(pool, "x1T", step_b)
                if has_prev(b):
                    wait_full(pool, "r", step_b - 1)
                for i in range(2):
                    pool.tensor_tensor(mixT[i][:, :], mix_cur[i][:, :], mix_prev[i][:, :], ALU.add).then_inc(mixed, 1)

            def squares(step_b):
                wait_read(pool, "kT", step_b)
                pool.tensor_tensor(kact[:, :], relu[:, :], relu[:, :], ALU.mult).then_inc(kact_done, 1)

            pool.memset(ident[:, :], 0.0).then_inc(consts_g, 1)
            pool.wait_ge(consts_g, 1)
            pool.affine_select(out=ident[:, :], in_=ident[:, :], compare_op=ALU.not_equal, fill=1.0, base=0,
                               pattern=[[-1, P]], channel_multiplier=1).then_inc(consts_g, 1)
            pool.memset(neg_one[:, :], -1.0).then_inc(consts_g, 1)
            pool.memset(zero_b[:, :], 0.0).then_inc(consts_g, 1)
            pool.memset(k_st[0][:, :, :].bitcast(U32), 0).then_inc(consts_g, 1)
            pool.memset(ident_b[:, :], 0.0).then_inc(consts_g, 1)
            pool.wait_ge(consts_g, 6)
            pool.affine_select(out=ident_b[:, :], in_=ident_b[:, :], compare_op=ALU.not_equal, fill=1.0, base=0,
                               pattern=[[-1, P]], channel_multiplier=1).then_inc(consts_g, 1)
            pool.memset(mask_b[:, :], 0.0).then_inc(consts_g, 1)
            pool.wait_ge(consts_g, 8)
            pool.affine_select(out=mask_b[:, :], in_=mask_b[:, :], compare_op=ALU.is_ge, fill=MASKED, base=0,
                               pattern=[[-1, P]], channel_multiplier=1).then_inc(consts_g, 1)
            pool.memset(vals[0][:, :, :, :], 0.0).then_inc(consts_g, 1)
            pool.wait_ge(consts_g, 10)
            pool.memset(vals[0][:, :, :, HD:HD + 1], 1.0).then_inc(consts_g, 1)
            lows(0)
            pool.memset(k_st[1][:, :, :].bitcast(U32), 0).then_inc(consts_g, 1)
            pool.memset(vals[1][:, :, :, :], 0.0).then_inc(consts_g, 1)
            pool.wait_ge(consts_g, 13)
            pool.memset(vals[1][:, :, :, HD:HD + 1], 1.0).then_inc(consts_g, 1)
            pool.memset(exponent[:, :], -0.5).then_inc(consts_g, 1)
            for i in range(2):
                pool.memset(mix_prev[i][:, 0:1], 0.0).then_inc(consts_g, 1)
            pool.wait_ge(consts_g, 17)
            wait_read(pool, "bp", -1)

            def body(b, par):
                for g in range(SLOTS):
                    if (g, has_prev(b)) == (2, True):
                        deviations(0, b - 1)
                    if g == 0 and (not fixed(b) or b >= 2):
                        deviations(1, b - 2)
                    zero_behind(b, g, 0)
                    if g == 0 and has_next(b):
                        lows(b + 1)
                    if g == 1:
                        residual_biased(b, par)
                    if (g, has_prev(b)) == (3, True):
                        squares(b)
                    zero_behind(b, g, 1)
                    if (g, has_prev(b)) == (2, True):
                        mix(b, b - 1)

            over_sequences(pool, body)

            last_b = NB - 1
            deviations(1, last_b - 1)
            deviations(0, last_b)
            mix(NB, last_b)
            squares(NB)
            deviations(1, last_b)


_INS = ["L0_attn_x", "L0_attn_w_attn", "L0_attn_b_attn", "L0_attn_w_proj", "L0_attn_b_proj",
        "L0_ffn_W_r", "L0_ffn_W_k", "L0_ffn_W_v", "L0_ffn_mu_r", "L0_ffn_mu_k"]


def kernel(**inputs):
    import numpy as _np
    import concourse.bacc as _bacc
    from concourse import mybir as _mybir
    from concourse.bass_utils import run_bass_kernel_spmd as _run

    nc = _bacc.Bacc("TRN2", target_bir_lowering=False, num_devices=1)
    arrays, args = {}, []
    for name in _INS:
        a = _np.ascontiguousarray(inputs[name])
        arrays[f"in_{name}_dram"] = a
        args.append(nc.dram_tensor(f"in_{name}_dram", a.shape, _mybir.dt.from_np(a.dtype), kind="ExternalInput").ap())
    shape = inputs["L0_attn_x"].shape
    args.append(nc.dram_tensor("out_0_dram", shape, _mybir.dt.float32, kind="ExternalOutput").ap())
    block_kernel(nc, *args)
    r = _run(nc, [arrays], core_ids=[0])
    return r.results[0]["out_0_dram"]
```

```python
from contextlib import ExitStack

import concourse.bass as bass
from concourse import mybir

F32 = mybir.dt.float32
BF16 = mybir.dt.bfloat16
U32 = mybir.dt.uint32
ALU = mybir.AluOpType
ACT = mybir.ActivationFunctionType
AX_X = mybir.AxisListType.X

P = 128
NB, T, C = 8, 512, 128
NH = 16
HD = C // NH
NT = T // P
HG = 4
SLOTS = NH // HG
SCALE = float(HD) ** -0.5
EPS = 1e-5
MASKED = -1e30

Q_PARTS = (0, 0, 0, 1, 1, 2)
K_PARTS = (0, 1, 2, 0, 1, 0)
MAX_ROW = len(Q_PARTS) * HD

VW = 32
PCOL = (0, 512, 1024, 896)
PW = 1280

EX_PAIR = ([(0, 0)], [(0, 1), (0, 3)], [(1, 0)], [(1, 1), (1, 3)], [(0, 2), (1, 2)])
MX_PAIR = ([(0, 3)], [(0, 2)], [(1, 3)], [(1, 2)], [(0, 1), (1, 1)], [(0, 0), (1, 0)])
EX_FILLS = [[(2 * p + h, t) for h, t in fill] for p in range(HG // 2) for fill in EX_PAIR]
MX_FILLS = [[(2 * p + h, t) for h, t in fill] for p in range(HG // 2) for fill in MX_PAIR]
EX_UNITS, MX_UNITS = len(EX_FILLS), len(MX_FILLS)
STEPS = MX_UNITS
EX_AT = {p * len(MX_PAIR) + i: p * len(EX_PAIR) + i for p in range(HG // 2) for i in range(len(EX_PAIR))}
Y_AT = (5, 4, 4, 7)
PV_AT = {2: 0, 5: 1, 8: 2, 11: 3}
MX_BANKS = 3
EX_BANKS = 2

SHARED_ORDER = (
    "maxT0 xT Y0 q k "
    "maxT1 Y1 ynT proj "
    "maxT2 Y2 v x1T "
    "maxT3 kT Y3 r kv"
).split()
HEAD_ORDER = "xT q k v wT bp maxT3".split()
TAIL_ORDER = "Y0 Y1 ynT proj x1T kT r kv".split()
SHARED_BANK = dict.fromkeys("maxT0 Y0 k Y1 proj Y2 x1T Y3 kv wT".split(), 0) | \
    dict.fromkeys("xT q maxT1 ynT maxT2 v maxT3 kT r bp".split(), 1)


def shared_uses():
    n, at = [0, 0], {}
    for name in HEAD_ORDER:
        n[SHARED_BANK[name]] += 1
        at[-1, name] = n[SHARED_BANK[name]]
    for b in range(NB):
        for name in SHARED_ORDER:
            prev_missing = b == 0 and name in ("Y0", "Y1", "ynT", "proj", "x1T", "kT", "r", "kv")
            next_missing = b == NB - 1 and name in ("xT", "q", "k", "v", "maxT3")
            if not (prev_missing or next_missing):
                n[SHARED_BANK[name]] += 1
                at[b, name] = n[SHARED_BANK[name]]
    for name in TAIL_ORDER:
        n[SHARED_BANK[name]] += 1
        at[NB, name] = n[SHARED_BANK[name]]
    return at


SHARED_USES = shared_uses()
LOOP_FROM, LOOP_TO = 2, 6


def shared_use(name, b):
    if isinstance(b, int):
        return SHARED_USES[b, name]
    first = SHARED_USES[LOOP_FROM, name]
    per = SHARED_USES[LOOP_FROM + 1, name] - first
    return (b - LOOP_FROM) * per + first


def wait(eng, sem, value):
    if not isinstance(value, int) or value > 0:
        eng.wait_ge(sem, value)


def wait_apart(eng, sem, value, passed):
    wait(eng, sem, value)
    if not isinstance(value, int):
        eng.sem_inc(passed, 1)


def block_kernel(nc, x, w_attn, b_attn, w_proj, b_proj, W_r, W_k, W_v, mu_r, mu_k, out):
    with ExitStack() as ctx:
        def sb(name, shape, dt=F32):
            return ctx.enter_context(nc.sbuf_tensor(name, shape, dt))

        def sem(name):
            return ctx.enter_context(nc.semaphore(name))

        ident = sb("ident", [P, P])
        ident_b = sb("ident_b", [P, P], BF16)
        mask_b = sb("mask_b", [P, P], BF16)
        neg_one = sb("neg_one", [2 * NH, T], BF16)
        zero_b = sb("zero_b", [2 * NH, T], BF16)
        w_in = sb("w_in", [P, 3 * C])
        w_q = sb("w_q", [P, C])
        w_k = sb("w_k", [P, C])
        w_o = sb("w_o", [P, C])
        w_ffn = sb("w_ffn", [P, 3, C])
        w_ffnT = sb("w_ffnT", [P, 3, C])
        b_q = sb("b_q", [P, 1])
        b_k = sb("b_k", [P, 1])
        b_v = sb("b_v", [P, 1])
        b_v_wide = sb("b_v_wide", [P, P])
        b_o = sb("b_o", [P, C])
        b_out = sb("b_out", [P, C])
        mu = [sb(f"mu{i}", [P, 1]) for i in range(2)]
        mu_rest = [sb(f"mu_rest{i}", [P, 1]) for i in range(2)]
        exponent = sb("exponent", [P, NT])

        x_in = [sb(f"x_in{i}", [P, NT, C]) for i in range(2)]
        x_res = [sb(f"x_res{i}", [P, NT, C]) for i in range(2)]
        xT = sb("xT", [P, T])
        q_part = sb("q_part", [P, 3, T], BF16)
        k_part = sb("k_part", [P, 3, T], BF16)
        q_rest = sb("q_rest", [P, T])
        k_rest = sb("k_rest", [P, T])
        q_st = [sb(f"q_st{i}", [P, NH, T], BF16) for i in range(2)]
        k_st = [sb(f"k_st{i}", [P, NH, T], BF16) for i in range(2)]
        vals = [sb(f"vals{i}", [P, NT, NH, VW]) for i in range(2)]
        yn = sb("yn", [P, NT, C])
        ynT = sb("ynT", [P, T])
        h1 = sb("h1", [P, NT, C])
        x1 = sb("x1", [P, NT, C])
        mix_cur = [sb(f"mix_cur{i}", [P, T]) for i in range(2)]
        mix_prev = [sb(f"mix_prev{i}", [P, T]) for i in range(2)]
        mixT = [sb(f"mixT{i}", [P, T]) for i in range(2)]
        gate = sb("gate", [P, NT, C])
        relu = sb("relu", [P, T])
        kact = sb("kact", [P, T])
        gated = sb("gated", [P, NT, C])
        h2 = sb("h2", [P, NT, C])
        o_sb = sb("o_sb", [P, NT, C])
        stats = [sb(f"stats{i}", [P, NT, 6]) for i in range(2)]
        mv = [sb(f"mv{i}", [P, NT, 2]) for i in range(2)]
        var_eps = [sb(f"var_eps{i}", [P, NT]) for i in range(2)]
        rstd = [sb(f"rstd{i}", [P, NT]) for i in range(2)]

        m_max = [sb(f"m_max{i}", [P, NT, HG]) for i in range(2)]
        m_part = sb("m_part", [P, NT, 2, HG], BF16)
        m_rows = sb("m_rows", [2 * HG, T], BF16)
        probs = [sb(f"probs{i}", [P, HG, PW]) for i in range(2)]
        yT = sb("yT", [P, T])
        rden = sb("rden", [P, NT, HG])

        def bank_of(name):
            return ctx.enter_context(nc.psum_tensor(name, [P, T], F32))

        mx_ps = [bank_of(f"mx_ps{i}") for i in range(MX_BANKS)]
        ex_ps = [bank_of(f"ex_ps{i}") for i in range(EX_BANKS)]
        pv_ps = bank_of("pv_ps")
        sh_ps = [bank_of(f"sh_ps{i}") for i in range(2)]

        w_in_loaded, w_loaded = sem("w_in_loaded"), sem("w_loaded")
        b_qk_loaded, vecs_loaded = sem("b_qk_loaded"), sem("vecs_loaded")
        xin_loaded = [sem(f"xin_loaded{i}") for i in range(2)]
        xres_loaded = [sem(f"xres_loaded{i}") for i in range(2)]
        consts_g = sem("consts_g")
        consts_v = sem("consts_v")
        ones_stacked = [sem(f"ones_stacked{i}") for i in range(2)]
        q_stacked, k_stacked = sem("q_stacked"), sem("k_stacked")
        rows_stacked = sem("rows_stacked")
        mx_full, mx_read = sem("mx_full"), sem("mx_read")
        ex_full, exp_done = sem("ex_full"), sem("exp_done")
        m_hi, m_parts = sem("m_hi"), sem("m_parts")
        causal = sem("causal")
        pv_done, yT_done, rden_done = sem("pv_done"), sem("yT_done"), sem("rden_done")
        sh_full = [sem(f"sh_full{i}") for i in range(2)]
        sh_read = [sem(f"sh_read{i}") for i in range(2)]
        high = [sem("q_high"), sem("k_high")]
        mid = [sem("q_mid"), sem("k_mid")]
        low = [sem("q_low"), sem("k_low")]
        xres_ready = sem("xres_ready")
        bn = [sem("bn1"), sem("bn2")]
        mean_var = [sem("mean_var1"), sem("mean_var2")]
        var_ready = [sem("var_ready1"), sem("var_ready2")]
        rstd_ready = [sem("rstd_ready1"), sem("rstd_ready2")]
        x1_done, o_done, h2_done = sem("x1_done"), sem("o_done"), sem("h2_done")
        key_shares, mixed = sem("key_shares"), sem("mixed")
        kact_done = sem("kact_done")
        stored = sem("stored")
        passed_v, passed_g, passed_s = sem("passed_v"), sem("passed_g"), sem("passed_s")

        x_d = x.rearrange("b (t p) c -> b p t c", p=P)
        out_d = out.rearrange("b (t p) c -> b p t c", p=P)
        Q_DMAS = 16 * (len(Q_PARTS) + 1)
        K_DMAS = 16 * len(K_PARTS)

        def fixed(b):
            return isinstance(b, int)

        def has_prev(b):
            return not fixed(b) or b >= 1

        def has_next(b):
            return not fixed(b) or b <= NB - 2

        def exists(b, g):
            return not fixed(b) or 0 <= SLOTS * b + g < NB * SLOTS

        def over_sequences(eng, body):
            for b in range(LOOP_FROM):
                body(b, b % 2)
            with eng.Fori(LOOP_FROM // 2, LOOP_TO // 2) as i:
                for par in range(2):
                    body(i * 2 + par, par)
            for b in range(LOOP_TO, NB):
                body(b, b % 2)

        def wait_full(eng, name, b):
            i = SHARED_BANK[name]
            wait(eng, sh_full[i], shared_use(name, b))
            return sh_ps[i], sh_read[i]

        def wait_read(eng, name, b):
            wait(eng, sh_read[SHARED_BANK[name]], shared_use(name, b))

        block = ctx.enter_context(nc.Block())

        @block.sync
        def _(sp):
            def stack(which, part, b, par):
                if part == 0:
                    wait_apart(sp, exp_done, (b - 1) * (SLOTS * EX_UNITS), passed_s)
                st, part_of, sem_of = ((q_st[par], q_part, q_stacked), (k_st[par], k_part, k_stacked))[which]
                wait(sp, (high, mid, low)[part][which], b + 1)
                for band, band_part in enumerate((Q_PARTS, K_PARTS)[which]):
                    if band_part == part:
                        sp.dma_start(st[band * HD:(band + 1) * HD, :, :], part_of[:, part, :]).then_inc(sem_of, 16)
                if which == 0 and part == 0:
                    sp.dma_start(st[MAX_ROW:MAX_ROW + 2, :, :], zero_b[:, :]).then_inc(q_stacked, 16)

            def stack_maxima(b, par, g, step_b, name):
                wait_read(sp, name, step_b)
                sp.dma_start(q_st[par][MAX_ROW:MAX_ROW + 2, g * HG:(g + 1) * HG, :],
                             m_rows[:, :]).then_inc(rows_stacked, 16)

            def store(b):
                wait(sp, o_done, b * NT + NT)
                sp.dma_start(out_d[b], o_sb[:, :, :]).then_inc(stored, 16)

            sp.dma_start(x_in[0][:, :, :], x_d[0]).then_inc(xin_loaded[0], 16)
            sp.dma_start(w_in[:, :], w_attn).then_inc(w_in_loaded, 16)
            sp.dma_start(b_q[:, :], b_attn[0:C].rearrange("(h d a) -> d h a", d=HD, a=1),
                         allow_slow_non_contiguous=True).then_inc(b_qk_loaded, 16)
            sp.dma_start(b_k[:, :], b_attn[C:2 * C].rearrange("(h d a) -> d h a", d=HD, a=1),
                         allow_slow_non_contiguous=True).then_inc(b_qk_loaded, 16)
            for w, wd in enumerate((W_r, W_k, W_v)):
                sp.dma_start(w_ffn[:, w, :], wd).then_inc(w_loaded, 16)
            sp.dma_start(w_o[:, :], w_proj).then_inc(w_loaded, 16)
            sp.dma_start(b_v[:, :], b_attn[2 * C:3 * C].rearrange("(p a) -> p a", a=1)).then_inc(vecs_loaded, 16)
            sp.dma_start(b_o[:, :], b_proj.partition_broadcast(P)).then_inc(vecs_loaded, 16)
            for i, m in enumerate((mu_r, mu_k)):
                sp.dma_start(mu[i][:, :], m.rearrange("(p a) -> p a", a=1)).then_inc(vecs_loaded, 16)
            sp.wait_ge(consts_g, 5)
            sp.dma_start(k_st[0][MAX_ROW:MAX_ROW + 2, :, :], neg_one[:, :]).then_inc(ones_stacked[0], 16)
            sp.wait_ge(consts_v, 1)
            for part in range(3):
                for which in range(2):
                    stack(which, part, 0, 0)
            sp.dma_start(x_in[1][:, :, :], x_d[1]).then_inc(xin_loaded[1], 16)
            sp.wait_ge(consts_g, 12)
            sp.dma_start(k_st[1][MAX_ROW:MAX_ROW + 2, :, :], neg_one[:, :]).then_inc(ones_stacked[1], 16)
            sp.wait_ge(consts_v, 7)
            stack_maxima(0, 0, 0, -1, "maxT3")

            def body(b, par):
                for g in range(SLOTS):
                    if g == 0:
                        if not fixed(b) or b >= 2:
                            wait_read(sp, "proj", b - 1)
                        sp.dma_start(x_res[par][:, :, :], x_d[b]).then_inc(xres_loaded[par], 16)
                    if exists(b, g + 1):
                        if g < SLOTS - 1:
                            stack_maxima(b, par, g + 1, b, f"maxT{g}")
                        else:
                            stack_maxima(b + 1, 1 - par, 0, b, f"maxT{g}")
                    if g == 0 and has_next(b):
                        for part in range(2):
                            for which in range(2):
                                stack(which, part, b + 1, 1 - par)
                    elif g == 1 and has_next(b):
                        for which in range(2):
                            stack(which, 2, b + 1, 1 - par)
                    if g == 2 and (not fixed(b) or b >= 2):
                        store(b - 2)
                    if g == 3 and (not fixed(b) or b + 2 < NB):
                        wait_read(sp, "xT", b - 1)
                        sp.dma_start(x_in[par][:, :, :], x_d[b + 2]).then_inc(xin_loaded[par], 16)

            over_sequences(sp, body)
            store(NB - 2)
            store(NB - 1)
            sp.wait_ge(stored, 16 * NB)

        @block.tensor
        def _(pe):
            mm = pe.matmul

            def bank(name, b):
                i = SHARED_BANK[name]
                wait(pe, sh_read[i], shared_use(name, b) - 1)
                return sh_ps[i], sh_full[i]

            def transpose4(name, b, src):
                ps, full = bank(name, b)
                for t in range(NT):
                    last = pe.transpose(ps[:, t * P:(t + 1) * P], src(t), ident[:, :])
                last.then_inc(full, 1)

            def product4(name, b, lhs, rhs):
                ps, full = bank(name, b)
                for t in range(NT):
                    last = mm(ps[:, t * P:(t + 1) * P], lhs[:, t * P:(t + 1) * P], rhs, start=True, stop=True)
                last.then_inc(full, 1)

            def product(name, b, lhs, rhs):
                ps, full = bank(name, b)
                mm(ps[:, :], lhs, rhs, start=True, stop=True).then_inc(full, 1)

            def x_transposed(step_b, b, par):
                wait(pe, xin_loaded[par], (b // 2 + 1) * 16 if fixed(b) else (b - par) * 8 + 16)
                transpose4("xT", step_b, lambda t: x_in[par][:, t, :])

            def queries(step_b):
                wait_read(pe, "xT", step_b)
                product("q", step_b, w_q[:, :], xT[:, :])

            def keys(step_b):
                product("k", step_b, w_k[:, :], xT[:, :])

            def values(step_b):
                product4("v", step_b, xT, w_in[:, 2 * C:3 * C])

            def maxima(b, par, g, u):
                if g == 0 and u == 0:
                    wait(pe, q_stacked, b * Q_DMAS + Q_DMAS)
                    wait(pe, k_stacked, b * K_DMAS + K_DMAS)
                wait(pe, mx_read, b * (SLOTS * MX_UNITS) + (g * MX_UNITS + u - MX_BANKS + 1))
                ps, at = mx_ps[u % MX_BANKS], 0
                for h, t in MX_FILLS[u]:
                    n, hd = (t + 1) * P, g * HG + h
                    mm(ps[:, at:at + n], q_st[par][:, hd, t * P:(t + 1) * P], k_st[par][:, hd, 0:n],
                       start=True, stop=False, skip_group_check=True)
                    at += n
                    last = mm(ps[:, at - P:at], ident_b[:, :], mask_b[:, :],
                              start=False, stop=True, skip_group_check=True)
                last.then_inc(mx_full, 1)

            def logits(b, par, g, u):
                if u == 0:
                    wait(pe, rows_stacked, b * (SLOTS * 16) + (g * 16 + 16))
                wait(pe, exp_done, b * (SLOTS * EX_UNITS) + (g * EX_UNITS + u - EX_BANKS + 1))
                ps, at = ex_ps[u % EX_BANKS], 0
                for h, t in EX_FILLS[u]:
                    n, hd = T - t * P, g * HG + h
                    last = mm(ps[:, at:at + n], k_st[par][:, hd, t * P:(t + 1) * P], q_st[par][:, hd, t * P:T],
                              start=True, stop=True)
                    at += n
                last.then_inc(ex_full, 1)

            def max_transposed(name, step_b, b, g):
                wait(pe, m_parts, b * SLOTS + (g + 1))
                ps, full = bank(name, step_b)
                for t in range(NT):
                    last = mm(ps[0:2 * HG, t * P:(t + 1) * P], m_part[:, t, :, :], ident_b[:, :],
                              start=True, stop=True)
                last.then_inc(full, 1)

            def weighted_values(b, par, g, t):
                wait(pe, causal, b * (SLOTS * 2 * NT) + (g * 2 * NT + NT + t + 1))
                if t == 0:
                    wait(pe, yT_done, b * SLOTS + g)
                if g == 0 and t == 0:
                    wait_read(pe, "v", b - 1)
                for h in range(HG):
                    last = mm(pv_ps[h * VW:(h + 1) * VW, t * P:T], vals[par][:, t, g * HG + h, :],
                              probs[g % 2][:, h, PCOL[t]:PCOL[t] + T - t * P],
                              start=(t == 0), stop=(t == NT - 1), skip_group_check=True)
                if t == NT - 1:
                    last.then_inc(pv_done, 1)

            def back_to_rows(name, step_b, b, g):
                wait(pe, yT_done, b * SLOTS + (g + 1))
                transpose4(name, step_b, lambda t: yT[:, t * P:(t + 1) * P])

            def attention_transposed(step_b):
                wait_read(pe, "Y1", step_b)
                transpose4("ynT", step_b, lambda t: yn[:, t, :])

            def project(step_b):
                wait_read(pe, "ynT", step_b)
                product4("proj", step_b, ynT, w_o[:, :])

            def x1_transposed(step_b, b):
                wait(pe, x1_done, b * NT + NT)
                transpose4("x1T", step_b, lambda t: x1[:, t, :])

            def ffn_in(step_b, b):
                wait(pe, mixed, b * 2 + 1)
                product("kT", step_b, w_ffnT[:, 1, :], mixT[1][:, :])

            def ffn_gate(step_b, b):
                wait(pe, mixed, b * 2 + 2)
                product4("r", step_b, mixT[0], w_ffnT[:, 0, :])

            def ffn_out(step_b, b):
                wait(pe, kact_done, b + 1)
                product4("kv", step_b, kact, w_ffnT[:, 2, :])

            pe.wait_ge(consts_g, 2)
            x_transposed(-1, 0, 0)
            pe.wait_ge(consts_v, 3)
            queries(-1)
            keys(-1)
            values(-1)
            pe.wait_ge(w_loaded, 64)
            ps, full = bank("wT", -1)
            for w in range(3):
                last = pe.transpose(ps[:, w * P:(w + 1) * P], w_ffn[:, w, :], ident[:, :])
            last.then_inc(full, 1)
            pe.wait_ge(consts_v, 4)
            ps, full = bank("bp", -1)
            mm(ps[:, 0:C], b_v_wide[:, :], w_o[:, :], start=True, stop=True).then_inc(full, 1)
            pe.wait_ge(consts_g, 9)
            pe.wait_ge(ones_stacked[0], 16)
            for u in range(MX_UNITS):
                maxima(0, 0, 0, u)
            for u in range(MX_UNITS):
                maxima(0, 0, 1, u)
                if u == 3:
                    max_transposed("maxT3", -1, 0, 0)
            pe.wait_ge(ones_stacked[1], 16)

            def body(b, par):
                for g in range(SLOTS):
                    for step in range(STEPS):
                        if step in EX_AT:
                            logits(b, par, g, EX_AT[step])
                        if exists(b, g + 2):
                            if g < 2:
                                maxima(b, par, g + 2, step)
                            else:
                                maxima(b + 1, 1 - par, g - 2, step)
                        if step in PV_AT and exists(b, g - 1):
                            if g:
                                weighted_values(b, par, g - 1, PV_AT[step])
                            else:
                                weighted_values(b - 1, 1 - par, SLOTS - 1, PV_AT[step])
                        if step == 3 and exists(b, g + 1):
                            max_transposed(f"maxT{g}", b, b, g + 1)
                        if step == Y_AT[g] and exists(b, g - 2):
                            back_to_rows(f"Y{g}", b, b, g - 2)
                        if has_next(b):
                            if (g, step) == (0, 4):
                                x_transposed(b, b + 1, 1 - par)
                            elif (g, step) == (0, 6):
                                queries(b)
                            elif (g, step) == (0, 8):
                                keys(b)
                            elif (g, step) == (2, 7):
                                values(b)
                        if has_prev(b):
                            if (g, step) == (1, 7):
                                attention_transposed(b)
                            elif (g, step) == (1, 11):
                                project(b)
                            elif (g, step) == (2, 11):
                                x1_transposed(b, b - 1)
                            elif (g, step) == (3, 6):
                                ffn_in(b, b - 1)
                            elif (g, step) == (3, 9):
                                ffn_gate(b, b - 1)
                            elif (g, step) == (3, 11):
                                ffn_out(b, b - 1)

            over_sequences(pe, body)

            last_b = NB - 1
            back_to_rows("Y0", NB, last_b, SLOTS - 2)
            for t in range(NT):
                weighted_values(last_b, last_b % 2, SLOTS - 1, t)
            back_to_rows("Y1", NB, last_b, SLOTS - 1)
            attention_transposed(NB)
            project(NB)
            x1_transposed(NB, last_b)
            ffn_in(NB, last_b)
            ffn_gate(NB, last_b)
            ffn_out(NB, last_b)

        @block.scalar
        def _(act):
            def copy(name, b, dst, cols=T):
                ps, read = wait_full(act, name, b)
                act.activation(dst, ps[0:dst.shape[0], 0:cols], ACT.Copy).then_inc(read, 1)

            def exps(b, g, u):
                if u == 0:
                    wait(act, pv_done, b * SLOTS + (g - 1))
                wait(act, ex_full, b * (SLOTS * EX_UNITS) + (g * EX_UNITS + u + 1))
                src = ex_ps[u % EX_BANKS][:, :]
                (h, t), *more = EX_FILLS[u]
                if (h + 1, t) in more:
                    src = src.rearrange("p (h q) -> p h q", h=2)
                    dst = probs[g % 2][:, h:h + 2, PCOL[t]:PCOL[t] + T - t * P]
                else:
                    dst = probs[g % 2][:, h, PCOL[t]:PCOL[t] + T]
                act.activation(dst, src, ACT.Exp, scale=SCALE).then_inc(exp_done, 1)

            def max_rows(name, step_b, n):
                wait(act, rows_stacked, n * 16)
                copy(name, step_b, m_rows[:, :])

            def sums(b, g):
                wait(act, pv_done, b * SLOTS + (g + 1))
                act.activation(yT[:, :], pv_ps[:, :], ACT.Copy).then_inc(yT_done, 1)

            q_and_k = (("q", q_part, q_rest, b_q), ("k", k_part, k_rest, b_k))

            def highs(i, step_b, b):
                name, part, _, bias = q_and_k[i]
                wait(act, (q_stacked, k_stacked)[i], b * (Q_DMAS, K_DMAS)[i])
                ps, _ = wait_full(act, name, step_b)
                act.activation(part[:, 0, :], ps[:, :], ACT.Identity, bias=bias[:, 0:1]).then_inc(high[i], 1)

            def mids(i, step_b, b):
                name, part, rest, _ = q_and_k[i]
                wait_read(act, name, step_b)
                act.activation(part[:, 1, :], rest[:, :], ACT.Copy).then_inc(mid[i], 1)

            def values(step_b, b, par):
                wait(act, pv_done, b * SLOTS - SLOTS)
                ps, read = wait_full(act, "v", step_b)
                act.activation(vals[par][:, :, :, 0:HD], ps[:, :].rearrange("p (t h d) -> p t h d", t=NT, h=NH),
                               ACT.Copy).then_inc(read, 1)

            def share(i, step_b, b):
                wait(act, mixed, b * 2)
                ps, read = wait_full(act, "x1T", step_b)
                m = 1 - i // 2
                if i % 2 == 0:
                    act.activation(mix_cur[m][:, :], ps[:, :], ACT.Copy, scale=mu[m][:, 0:1])
                else:
                    act.activation(mix_prev[m][:, 1:T], ps[:, 0:T - 1], ACT.Copy, scale=mu_rest[m][:, 0:1]
                                   ).then_inc(key_shares if i == 1 else read, 1)

            def rectify(step_b):
                ps, read = wait_full(act, "kT", step_b)
                act.activation(relu[:, :], ps[:, :], ACT.Relu).then_inc(read, 1)

            def gates(step_b):
                ps, read = wait_full(act, "r", step_b)
                act.activation(gate[:, :, :], ps[:, :].rearrange("p (t c) -> p t c", t=NT), ACT.Tanh, scale=0.5
                               ).then_inc(read, 1)

            copy("xT", -1, xT[:, :])
            act.wait_ge(b_qk_loaded, 32)
            highs(0, -1, 0)
            highs(1, -1, 0)
            mids(0, -1, 0)
            mids(1, -1, 0)
            act.wait_ge(consts_g, 11)
            values(-1, 0, 0)
            copy("wT", -1, w_ffnT[:, :, :].rearrange("p w c -> p (w c)"), 3 * C)
            max_rows("maxT3", -1, 0)
            act.wait_ge(consts_g, 14)
            act.wait_ge(consts_v, 6)

            def body(b, par):
                for g in range(SLOTS):
                    for step in range(STEPS):
                        if step in EX_AT:
                            exps(b, g, EX_AT[step])
                        if step == 0 and exists(b, g - 2):
                            if exists(b, g - 3):
                                if g:
                                    wait_read(act, f"Y{g - 1}", b)
                                else:
                                    wait_read(act, "Y3", b - 1)
                            sums(b, g - 2)
                        if step == 4 and exists(b, g + 1):
                            max_rows(f"maxT{g}", b, b * SLOTS + (g + 1))
                        if has_next(b):
                            if (g, step) == (0, 5):
                                copy("xT", b, xT[:, :])
                            elif (g, step) in ((0, 7), (0, 9)):
                                highs((step - 7) // 2, b, b + 1)
                            elif (g, step) in ((0, 10), (1, 1)):
                                mids(g, b, b + 1)
                            elif (g, step) == (2, 8):
                                values(b, b + 1, 1 - par)
                        if has_prev(b):
                            if (g, step) == (1, 8):
                                copy("ynT", b, ynT[:, :])
                            elif g == 3 and 1 <= step <= 5 and step != 4:
                                share((1, 2, 3, 5).index(step), b, b - 1)
                            elif (g, step) == (3, 7):
                                rectify(b)
                            elif (g, step) == (3, 10):
                                gates(b)

            over_sequences(act, body)

            last_b = NB - 1
            wait_read(act, "Y3", last_b)
            sums(last_b, SLOTS - 2)
            wait_read(act, "Y0", NB)
            sums(last_b, SLOTS - 1)
            copy("ynT", NB, ynT[:, :])
            for i in range(4):
                share(i, NB, last_b)
            rectify(NB)
            gates(NB)

        @block.vector
        def _(dve):
            def reduce_maxima(b, g, u):
                wait(dve, mx_full, b * (SLOTS * MX_UNITS) + (g * MX_UNITS + u + 1))
                (h, t), *more = MX_FILLS[u]
                heads, n = 1 + len(more), (t + 1) * P
                src = mx_ps[u % MX_BANKS][:, 0:n * heads].rearrange("p (h k) -> p h k", h=heads)
                dve.tensor_reduce(m_max[g % 2][:, t, h:h + heads], src, AX_X, ALU.max).then_inc(mx_read, 1)

            def max_parts(b, g, before, before_b):
                s, m = b * SLOTS + g, m_max[g % 2]
                wait(dve, mx_read, b * (SLOTS * MX_UNITS) + (g + 1) * MX_UNITS)
                if before:
                    wait_full(dve, before, before_b)
                dve.tensor_copy(m_part[:, :, 0, :], m[:, :, :]).then_inc(m_hi, 1)
                wait(dve, m_hi, s + 1)
                dve.tensor_tensor(m_part[:, :, 1, :], m[:, :, :], m_part[:, :, 0, :], ALU.subtract).then_inc(m_parts, 1)

            def rests(i, step_b, b):
                name, part, rest, bias = (("q", q_part, q_rest, b_q), ("k", k_part, k_rest, b_k))[i]
                wait(dve, high[i], b + 1)
                wait(dve, low[i], b)
                ps, read = wait_full(dve, name, step_b)
                dve.scalar_tensor_tensor(out=rest[:, :], in0=ps[:, :], scalar=bias[:, 0:1], in1=part[:, 0, :],
                                         op0=ALU.add, op1=ALU.subtract).then_inc(read, 1)

            def normalise(name, step_b, b, g):
                ps, read = wait_full(dve, name, step_b)
                y = ps[:, :].rearrange("p (t h w) -> p t h w", t=NT, h=HG)
                dve.reciprocal(rden[:, :, :], y[:, :, :, HD]).then_inc(rden_done, 1)
                wait(dve, rden_done, b * SLOTS + (g + 1))
                if g == 0 and has_prev(b):
                    wait_full(dve, "ynT", step_b)
                dst = yn[:, :, g * HG * HD:(g + 1) * HG * HD].rearrange("p t (h d) -> p t h d", h=HG)
                dve.tensor_tensor(dst, y[:, :, :, 0:HD], rden[:, :, :].unsqueeze(3).to_broadcast([P, NT, HG, HD]),
                                  ALU.mult).then_inc(read, 1)

            def statistics(i, b, src):
                wait(dve, rstd_ready[i], b)
                for t in range(NT):
                    dve.bn_stats(stats[i][:, t, :], src[:, t, :]).then_inc(bn[i], 1)
                wait_apart(dve, bn[i], b * NT + NT, passed_v)
                for t in range(NT):
                    dve.bn_aggr(mv[i][:, t, :], stats[i][:, t, :]).then_inc(mean_var[i], 1)

            def normed(i, b, src, dst, done):
                wait(dve, rstd_ready[i], b + 1)
                for t in range(NT):
                    dve.tensor_scalar(dst[:, t, :], src[:, t, :], mv[i][:, t, 0:1], rstd[i][:, t:t + 1],
                                      ALU.subtract, ALU.mult).then_inc(done, 1)

            def attention_added(step_b, b, par):
                wait(dve, xres_ready, b + 1)
                wait(dve, x1_done, b * NT)
                ps, read = wait_full(dve, "proj", step_b)
                dve.tensor_tensor(h1[:, :, :], ps[:, :].rearrange("p (t c) -> p t c", t=NT), x_res[par][:, :, :],
                                  ALU.add).then_inc(read, 1)

            def attention_statistics(step_b, b):
                wait_read(dve, "proj", step_b)
                statistics(0, b, h1)

            def attention_normed(step_b, b):
                wait(dve, h2_done, b)
                normed(0, b, h1, x1, x1_done)

            def ffn_added(step_b, b):
                wait(dve, o_done, b * NT)
                ps, read = wait_full(dve, "kv", step_b)
                wait_read(dve, "r", step_b)
                dve.scalar_tensor_tensor(out=gated[:, :, :], in0=gate[:, :, :], scalar=1.0,
                                         in1=ps[:, :].rearrange("p (t c) -> p t c", t=NT),
                                         op0=ALU.add, op1=ALU.mult).then_inc(read, 1)
                wait_read(dve, "kv", step_b)
                dve.scalar_tensor_tensor(out=h2[:, :, :], in0=gated[:, :, :], scalar=0.5, in1=x1[:, :, :],
                                         op0=ALU.mult, op1=ALU.add).then_inc(h2_done, 1)

            def ffn_statistics(b):
                wait(dve, h2_done, b + 1)
                statistics(1, b, h2)

            def ffn_normed(b):
                wait(dve, stored, b * 16)
                normed(1, b, h2, o_sb, o_done)

            dve.memset(q_st[0][:, :, :].bitcast(U32), 0).then_inc(consts_v, 1)
            dve.wait_ge(w_in_loaded, 16)
            for i, w in enumerate((w_q, w_k)):
                dve.tensor_copy(w[:, :].rearrange("p (d h) -> p d h", d=HD),
                                w_in[:, i * C:(i + 1) * C].rearrange("p (h d) -> p d h", d=HD)).then_inc(consts_v, 1)
            dve.wait_ge(vecs_loaded, 64)
            dve.tensor_copy(b_v_wide[:, :], b_v[:, 0:1].to_broadcast([P, P])).then_inc(consts_v, 1)
            for i in range(2):
                dve.tensor_scalar(mu_rest[i][:, :], mu[i][:, :], -1.0, 1.0, ALU.mult, ALU.add).then_inc(consts_v, 1)
            dve.wait_ge(b_qk_loaded, 32)
            rests(0, -1, 0)
            rests(1, -1, 0)
            dve.memset(q_st[1][:, :, :].bitcast(U32), 0).then_inc(consts_v, 1)
            ps, read = wait_full(dve, "bp", -1)
            dve.tensor_tensor(b_out[:, :], ps[:, 0:C], b_o[:, :], ALU.add).then_inc(read, 1)
            for g in range(2):
                for u in range(MX_UNITS):
                    reduce_maxima(0, g, u)
                max_parts(0, g, "maxT3" if g else None, -1)

            def body(b, par):
                for g in range(SLOTS):
                    for step in range(STEPS):
                        if exists(b, g + 2):
                            if g < 2:
                                reduce_maxima(b, g + 2, step)
                            else:
                                reduce_maxima(b + 1, g - 2, step)
                        if step == Y_AT[g] + 1 and exists(b, g - 2):
                            if g < 2:
                                normalise(f"Y{g}", b, b - 1, g + 2)
                            else:
                                normalise(f"Y{g}", b, b, g - 2)
                        if has_next(b) and (g, step) in ((0, 8), (0, 10)):
                            rests((step - 8) // 2, b, b + 1)
                        if not fixed(b) or b >= 2:
                            if (g, step) == (0, 0):
                                ffn_added(b - 1, b - 2)
                            elif (g, step) == (0, 2):
                                ffn_statistics(b - 2)
                            elif (g, step) == (1, 2):
                                ffn_normed(b - 2)
                        if has_prev(b):
                            if (g, step) == (1, 11):
                                attention_added(b, b - 1, 1 - par)
                            elif (g, step) == (2, 0):
                                attention_statistics(b, b - 1)
                            elif (g, step) == (2, 8):
                                attention_normed(b, b - 1)
                    if exists(b, g + 2):
                        if g < 2:
                            max_parts(b, g + 2, f"maxT{g}", b)
                        else:
                            max_parts(b + 1, g - 2, f"maxT{g}", b)

            over_sequences(dve, body)

            last_b = NB - 1
            ffn_added(last_b, last_b - 1)
            ffn_statistics(last_b - 1)
            ffn_normed(last_b - 1)
            normalise("Y0", NB, last_b, SLOTS - 2)
            normalise("Y1", NB, last_b, SLOTS - 1)
            attention_added(NB, last_b, last_b % 2)
            attention_statistics(NB, last_b)
            attention_normed(NB, last_b)
            ffn_added(NB, last_b)
            ffn_statistics(last_b)
            ffn_normed(last_b)

        @block.gpsimd
        def _(pool):
            def zero_behind(b, g, pair):
                wait_apart(pool, exp_done, b * (SLOTS * EX_UNITS) + (g * EX_UNITS + 5 * pair + 5), passed_g)
                for t in range(NT):
                    blocks = probs[g % 2][:, 2 * pair:2 * pair + 2, PCOL[t]:PCOL[t] + P]
                    pool.affine_select(out=blocks, in_=blocks, compare_op=ALU.is_ge, fill=0.0, base=0,
                                       pattern=[[0, 2], [1, P]], channel_multiplier=-1).then_inc(causal, 1)

            def lows(b):
                for i, (part, rest) in enumerate(((q_part, q_rest), (k_part, k_rest))):
                    wait(pool, mid[i], b + 1)
                    pool.tensor_tensor(part[:, 2, :], rest[:, :], part[:, 1, :], ALU.subtract).then_inc(low[i], 1)

            def residual_biased(b, par):
                wait(pool, xres_loaded[par], (b // 2 + 1) * 16 if fixed(b) else (b - par) * 8 + 16)
                pool.tensor_tensor(x_res[par][:, :, :], x_res[par][:, :, :],
                                   b_out[:, :].unsqueeze(1).to_broadcast([P, NT, C]), ALU.add).then_inc(xres_ready, 1)

            def deviations(i, b):
                wait(pool, mean_var[i], b * NT + NT)
                wait_apart(pool, (x1_done, o_done)[i], b * NT, passed_g)
                pool.tensor_scalar(var_eps[i][:, :], mv[i][:, :, 1], EPS, None, ALU.add).then_inc(var_ready[i], 1)
                wait(pool, var_ready[i], b + 1)
                pool.tensor_tensor(rstd[i][:, :], var_eps[i][:, :], exponent[:, :], ALU.pow).then_inc(rstd_ready[i], 1)

            def mix(step_b, b):
                if has_prev(b):
                    wait_full(pool, "r", step_b - 1)
                wait(pool, key_shares, b + 1)
                pool.tensor_tensor(mixT[1][:, :], mix_cur[1][:, :], mix_prev[1][:, :], ALU.add).then_inc(mixed, 1)
                wait_read(pool, "x1T", step_b)
                pool.tensor_tensor(mixT[0][:, :], mix_cur[0][:, :], mix_prev[0][:, :], ALU.add).then_inc(mixed, 1)

            def squares(step_b):
                wait_read(pool, "kT", step_b)
                pool.tensor_tensor(kact[:, :], relu[:, :], relu[:, :], ALU.mult).then_inc(kact_done, 1)

            pool.memset(ident[:, :], 0.0).then_inc(consts_g, 1)
            pool.wait_ge(consts_g, 1)
            pool.affine_select(out=ident[:, :], in_=ident[:, :], compare_op=ALU.not_equal, fill=1.0, base=0,
                               pattern=[[-1, P]], channel_multiplier=1).then_inc(consts_g, 1)
            pool.memset(neg_one[:, :], -1.0).then_inc(consts_g, 1)
            pool.memset(zero_b[:, :], 0.0).then_inc(consts_g, 1)
            pool.memset(k_st[0][:, :, :].bitcast(U32), 0).then_inc(consts_g, 1)
            pool.memset(ident_b[:, :], 0.0).then_inc(consts_g, 1)
            pool.wait_ge(consts_g, 6)
            pool.affine_select(out=ident_b[:, :], in_=ident_b[:, :], compare_op=ALU.not_equal, fill=1.0, base=0,
                               pattern=[[-1, P]], channel_multiplier=1).then_inc(consts_g, 1)
            pool.memset(mask_b[:, :], 0.0).then_inc(consts_g, 1)
            pool.wait_ge(consts_g, 8)
            pool.affine_select(out=mask_b[:, :], in_=mask_b[:, :], compare_op=ALU.is_ge, fill=MASKED, base=0,
                               pattern=[[-1, P]], channel_multiplier=1).then_inc(consts_g, 1)
            pool.memset(vals[0][:, :, :, :], 0.0).then_inc(consts_g, 1)
            pool.wait_ge(consts_g, 10)
            pool.memset(vals[0][:, :, :, HD:HD + 1], 1.0).then_inc(consts_g, 1)
            lows(0)
            pool.memset(k_st[1][:, :, :].bitcast(U32), 0).then_inc(consts_g, 1)
            pool.memset(vals[1][:, :, :, :], 0.0).then_inc(consts_g, 1)
            pool.wait_ge(consts_g, 13)
            pool.memset(vals[1][:, :, :, HD:HD + 1], 1.0).then_inc(consts_g, 1)
            pool.memset(exponent[:, :], -0.5).then_inc(consts_g, 1)
            for i in range(2):
                pool.memset(mix_prev[i][:, 0:1], 0.0).then_inc(consts_g, 1)
            pool.wait_ge(consts_g, 17)
            wait_read(pool, "bp", -1)

            def body(b, par):
                for g in range(SLOTS):
                    if g == 0 and (not fixed(b) or b >= 2):
                        deviations(1, b - 2)
                    if g == 1 and has_next(b):
                        lows(b + 1)
                    if g == 1:
                        residual_biased(b, par)
                    if (g, has_prev(b)) == (2, True):
                        deviations(0, b - 1)
                    if (g, has_prev(b)) == (3, True):
                        mix(b, b - 1)
                    zero_behind(b, g, 0)
                    if (g, has_prev(b)) == (3, True):
                        squares(b)
                    zero_behind(b, g, 1)

            over_sequences(pool, body)

            last_b = NB - 1
            deviations(1, last_b - 1)
            deviations(0, last_b)
            mix(NB, last_b)
            squares(NB)
            deviations(1, last_b)


_INS = ["L0_attn_x", "L0_attn_w_attn", "L0_attn_b_attn", "L0_attn_w_proj", "L0_attn_b_proj",
        "L0_ffn_W_r", "L0_ffn_W_k", "L0_ffn_W_v", "L0_ffn_mu_r", "L0_ffn_mu_k"]


def kernel(**inputs):
    import numpy as _np
    import concourse.bacc as _bacc
    from concourse import mybir as _mybir
    from concourse.bass_utils import run_bass_kernel_spmd as _run

    nc = _bacc.Bacc("TRN2", target_bir_lowering=False, num_devices=1)
    arrays, args = {}, []
    for name in _INS:
        a = _np.ascontiguousarray(inputs[name])
        arrays[f"in_{name}_dram"] = a
        args.append(nc.dram_tensor(f"in_{name}_dram", a.shape, _mybir.dt.from_np(a.dtype), kind="ExternalInput").ap())
    shape = inputs["L0_attn_x"].shape
    args.append(nc.dram_tensor("out_0_dram", shape, _mybir.dt.float32, kind="ExternalOutput").ap())
    block_kernel(nc, *args)
    r = _run(nc, [arrays], core_ids=[0])
    return r.results[0]["out_0_dram"]
```

```python
from contextlib import ExitStack

import concourse.bass as bass
from concourse import mybir

F32 = mybir.dt.float32
BF16 = mybir.dt.bfloat16
U32 = mybir.dt.uint32
ALU = mybir.AluOpType
ACT = mybir.ActivationFunctionType

P = 128
NB, T, C = 8, 512, 128
NH = 16
HD = C // NH
NT = T // P
HG = 4
SLOTS = NH // HG
SCALE = float(HD) ** -0.5
EPS = 1e-5
LOWEST = -3.4e38
MASKED = -1e30

Q_PARTS = (0, 0, 0, 1, 1, 2)
K_PARTS = (0, 1, 2, 0, 1, 0)
MAX_ROW = len(Q_PARTS) * HD

PAIRS = SLOTS // 2
VW = 32
PCOL = (0, 512, 1024, 896)
PW = 1280

EX_PAIR = ([(0, 1), (0, 3)], [(1, 0)], [(0, 0)], [(0, 2), (1, 2)], [(1, 1), (1, 3)])
MX_PAIR = ([(0, 2)], [(0, 3)], [(1, 3)], [(0, 0), (1, 0)], [(1, 2)], [(0, 1), (1, 1)])
EX_FILLS = [[(2 * p + h, t) for h, t in fill] for p in range(HG // 2) for fill in EX_PAIR]
MX_FILLS = [[(2 * p + h, t) for h, t in fill] for p in range(HG // 2) for fill in MX_PAIR]
EX_UNITS, MX_UNITS = len(EX_FILLS), len(MX_FILLS)
STEPS = MX_UNITS
NO_EX = (7, 8)
EX_AT = {step: u for u, step in enumerate(s for s in range(STEPS) if s not in NO_EX)}
PV_AT = {1: 0, 3: 1, 7: 2, 9: 3}
PE_AT = {"maxT0": 2, "xT": 4, "q": 7, "k": 10, "Y1": 12, "maxT1": 16, "ynT": 17, "proj": 20, "v": 23, "maxT2": 26,
         "x1T": 30, "Y0": 35, "kT": 38, "maxT3": 41, "r": 42, "kv": 44}
ACT_AT = {"maxT0": 2, "xT": 4, "q": 6, "sums1": 9, "k": 11, "q_mid": 12, "k_mid": 15, "maxT1": 16, "ynT": 16, "norm2":
          20, "norm2b": 23, "v": 25, "maxT2": 26, "share0": 31, "share1": 32, "sums0": 33, "share2": 36, "share3": 37,
          "kT": 38, "maxT3": 40, "r": 41}
DVE_AT = {"aggregates2": 0, "q": 10, "Y1": 11, "k": 12, "add1": 20, "stats1": 22, "stats1b": 22, "aggregates1": 23,
          "norm1b": 26, "norm1": 27, "Y0": 35, "gated": 44, "add2": 46, "stats2": 47, "stats2b": 47}
POOL_AT = {"deviations2": 0, "residual": 1, "q_low": 2, "k_low": 3, "deviations1": 6, "mix1": 7, "mix0": 9, "squares":
           9}
MX_BANKS = 3
EX_BANKS = 2


def head_of(g, h):
    return h * SLOTS + g


SHARED_ORDER = sorted(PE_AT, key=PE_AT.get)
HEAD_ORDER = "xT q k v wT bp maxT3".split()
TAIL_ORDER = ["Y1"]
SHARED_BANK = dict.fromkeys("maxT0 xT q Y1 maxT1 proj v maxT2 Y0 kT maxT3 kv wT".split(), 0) | \
    dict.fromkeys("k ynT x1T r bp".split(), 1)


def shared_uses():
    n, at = [0, 0], {}
    for name in HEAD_ORDER:
        n[SHARED_BANK[name]] += 1
        at[-1, name] = n[SHARED_BANK[name]]
    for b in range(NB):
        for name in SHARED_ORDER:
            prev_missing = b == 0 and name in ("Y1", "ynT", "proj", "x1T", "kT", "r", "kv")
            next_missing = b == NB - 1 and name in ("xT", "q", "k", "v", "maxT3")
            if not (prev_missing or next_missing):
                n[SHARED_BANK[name]] += 1
                at[b, name] = n[SHARED_BANK[name]]
    for name in TAIL_ORDER:
        n[SHARED_BANK[name]] += 1
        at[NB, name] = n[SHARED_BANK[name]]
    return at


SHARED_USES = shared_uses()
LOOP_FROM, LOOP_TO = 2, 6


def shared_use(name, b):
    if isinstance(b, int):
        return SHARED_USES[b, name]
    first = SHARED_USES[LOOP_FROM, name]
    per = SHARED_USES[LOOP_FROM + 1, name] - first
    return (b - LOOP_FROM) * per + first


def wait(eng, sem, value):
    if not isinstance(value, int) or value > 0:
        eng.wait_ge(sem, value)


def wait_apart(eng, sem, value, passed):
    wait(eng, sem, value)
    if not isinstance(value, int):
        eng.sem_inc(passed, 1)


def block_kernel(nc, x, w_attn, b_attn, w_proj, b_proj, W_r, W_k, W_v, mu_r, mu_k, out):
    with ExitStack() as ctx:
        def sb(name, shape, dt=F32):
            return ctx.enter_context(nc.sbuf_tensor(name, shape, dt))

        def sem(name):
            return ctx.enter_context(nc.semaphore(name))

        ident = sb("ident", [P, P])
        ident_b = sb("ident_b", [P, P], BF16)
        mask_wide = sb("mask_wide", [P, T])
        neg_one = sb("neg_one", [2 * NH, T], BF16)
        zero_b = sb("zero_b", [2 * NH, T], BF16)
        w_in = sb("w_in", [P, 3 * C])
        w_q = sb("w_q", [P, C])
        w_k = sb("w_k", [P, C])
        w_o = sb("w_o", [P, C])
        w_ffn = sb("w_ffn", [P, 3, C])
        w_ffnT = sb("w_ffnT", [P, 3, C])
        b_q = sb("b_q", [P, 1])
        b_k = sb("b_k", [P, 1])
        b_v = sb("b_v", [P, 1])
        b_v_wide = sb("b_v_wide", [P, P])
        b_o = sb("b_o", [P, C])
        b_out = sb("b_out", [P, C])
        mu = [sb(f"mu{i}", [P, 1]) for i in range(2)]
        mu_rest = [sb(f"mu_rest{i}", [P, 1]) for i in range(2)]
        exponent = sb("exponent", [P, NT])

        x_in = [sb(f"x_in{i}", [P, NT, C]) for i in range(2)]
        x_res = [sb(f"x_res{i}", [P, NT, C]) for i in range(2)]
        xT = sb("xT", [P, T])
        q_part = sb("q_part", [P, 3, T], BF16)
        k_part = sb("k_part", [P, 3, T], BF16)
        q_rest = sb("q_rest", [P, T])
        k_rest = sb("k_rest", [P, T])
        q_st = [sb(f"q_st{i}", [P, NH, T], BF16) for i in range(2)]
        k_st = [sb(f"k_st{i}", [P, NH, T], BF16) for i in range(2)]
        vals = [sb(f"vals{i}", [P, NT, NH, VW]) for i in range(2)]
        yn = sb("yn", [P, NT, C])
        ynT = sb("ynT", [P, T])
        h1 = sb("h1", [P, NT, C])
        x1 = sb("x1", [P, NT, C])
        mix_cur = [sb(f"mix_cur{i}", [P, T]) for i in range(2)]
        mix_prev = [sb(f"mix_prev{i}", [P, T]) for i in range(2)]
        mixT = [sb(f"mixT{i}", [P, T]) for i in range(2)]
        gate = sb("gate", [P, NT, C])
        relu = sb("relu", [P, T])
        kact = sb("kact", [P, T])
        gated = sb("gated", [P, NT, C])
        h2 = sb("h2", [P, NT, C])
        o_sb = sb("o_sb", [P, NT, C])
        stats = [sb(f"stats{i}", [P, NT, 6]) for i in range(2)]
        mv = [sb(f"mv{i}", [P, NT, 2]) for i in range(2)]
        var_eps = [sb(f"var_eps{i}", [P, NT]) for i in range(2)]
        rstd = [sb(f"rstd{i}", [P, NT]) for i in range(2)]
        neg_mean = sb("neg_mean", [P, NT])
        shift = sb("shift", [P, NT])

        m_max = [sb(f"m_max{i}", [P, NT, HG]) for i in range(2)]
        masked = [sb(f"masked{i}", [P, T]) for i in range(len(MX_PAIR))]
        m_part = sb("m_part", [P, NT, 2, HG], BF16)
        m_rows = sb("m_rows", [2 * HG, T], BF16)
        probs = [sb(f"probs{i}", [P, HG, PW]) for i in range(2)]
        yT = sb("yT", [P, T])
        rden = sb("rden", [P, NT, HG, 2])

        def bank_of(name):
            return ctx.enter_context(nc.psum_tensor(name, [P, T], F32))

        mx_ps = [bank_of(f"mx_ps{i}") for i in range(MX_BANKS)]
        ex_ps = [bank_of(f"ex_ps{i}") for i in range(EX_BANKS)]
        pv_ps = bank_of("pv_ps")
        sh_ps = [bank_of(f"sh_ps{i}") for i in range(2)]

        w_in_loaded, w_loaded = sem("w_in_loaded"), sem("w_loaded")
        b_qk_loaded, vecs_loaded = sem("b_qk_loaded"), sem("vecs_loaded")
        xin_loaded = [sem(f"xin_loaded{i}") for i in range(2)]
        xres_loaded = [sem(f"xres_loaded{i}") for i in range(2)]
        consts_g = sem("consts_g")
        mask_ready = sem("mask_ready")
        consts_v = sem("consts_v")
        ones_stacked = [sem(f"ones_stacked{i}") for i in range(2)]
        q_stacked, k_stacked = sem("q_stacked"), sem("k_stacked")
        rows_stacked = sem("rows_stacked")
        mx_full, mx_read = sem("mx_full"), sem("mx_read")
        ex_full, exp_done = sem("ex_full"), sem("exp_done")
        m_hi, m_parts = sem("m_hi"), sem("m_parts")
        causal = sem("causal")
        pv_done, yT_done, rden_done = sem("pv_done"), sem("yT_done"), sem("rden_done")
        sh_full = [sem(f"sh_full{i}") for i in range(2)]
        sh_read = [sem(f"sh_read{i}") for i in range(2)]
        high = [sem("q_high"), sem("k_high")]
        mid = [sem("q_mid"), sem("k_mid")]
        low = [sem("q_low"), sem("k_low")]
        xres_ready = sem("xres_ready")
        bn = [sem("bn1"), sem("bn2")]
        mean_var = [sem("mean_var1"), sem("mean_var2")]
        var_ready = [sem("var_ready1"), sem("var_ready2")]
        rstd_ready = [sem("rstd_ready1"), sem("rstd_ready2")]
        neg_mean_ready, shift_ready = sem("neg_mean_ready"), sem("shift_ready")
        x1_done, o_done, h2_done = sem("x1_done"), sem("o_done"), sem("h2_done")
        key_shares, mixed = sem("key_shares"), sem("mixed")
        kact_done = sem("kact_done")
        stored = sem("stored")
        yn_half, ynT_half, proj_half = sem("yn_half"), sem("ynT_half"), sem("proj_half")
        ynT_copied, h1_half, x1T_half = sem("ynT_copied"), sem("h1_half"), sem("x1T_half")
        prev_half, mixed_half, kT_half = sem("prev_half"), sem("mixed_half"), sem("kT_half")
        relu_half = sem("relu_half")
        kact_half, r_half, gate_half = sem("kact_half"), sem("r_half"), sem("gate_half")
        kv_half, gated_half, h2_half = sem("kv_half"), sem("gated_half"), sem("h2_half")
        passed_v, passed_g, passed_s = sem("passed_v"), sem("passed_g"), sem("passed_s")

        x_d = x.rearrange("b (t p) c -> b p t c", p=P)
        out_d = out.rearrange("b (t p) c -> b p t c", p=P)
        Q_DMAS = 16 * (len(Q_PARTS) + 1)
        K_DMAS = 16 * len(K_PARTS)

        def fixed(b):
            return isinstance(b, int)

        def has_prev(b):
            return not fixed(b) or b >= 1

        def has_next(b):
            return not fixed(b) or b <= NB - 2

        def exists(b, g):
            return not fixed(b) or 0 <= SLOTS * b + g < NB * SLOTS

        def over_sequences(eng, body):
            for b in range(LOOP_FROM):
                body(b, b % 2)
            with eng.Fori(LOOP_FROM // 2, LOOP_TO // 2) as i:
                for par in range(2):
                    body(i * 2 + par, par)
            for b in range(LOOP_TO, NB):
                body(b, b % 2)

        def ex_bank(b, g, u):
            deep = fixed(b) and b == NB - 1 and g >= SLOTS - 2
            banks = ex_ps + mx_ps if deep else ex_ps
            before = EX_BANKS if deep and g == SLOTS - 2 and u < EX_BANKS else len(banks)
            return banks[u % len(banks)], before

        def wait_full(eng, name, b):
            i = SHARED_BANK[name]
            wait(eng, sh_full[i], shared_use(name, b))
            return sh_ps[i], sh_read[i]

        def wait_read(eng, name, b):
            wait(eng, sh_read[SHARED_BANK[name]], shared_use(name, b))

        ynT_ps = x1T_ps = kv_ps = [mx_ps[0], ex_ps[0]]
        proj_ps = kT_ps = [mx_ps[1], ex_ps[1]]
        r_ps = [mx_ps[2], pv_ps]
        HALF = T // 2
        half_tiles = lambda half: range(half * NT // 2, (half + 1) * NT // 2)
        half_cols = lambda half: slice(half * HALF, (half + 1) * HALF)
        in_bank = lambda t: slice(t * P % HALF, t * P % HALF + P)

        block = ctx.enter_context(nc.Block())

        @block.sync
        def _(sp):
            def stack(which, part, b, par):
                if part == 0:
                    wait_apart(sp, exp_done, (b - 1) * (SLOTS * EX_UNITS), passed_s)
                if which == 0 and part == 0:
                    sp.dma_start(q_st[par][MAX_ROW:MAX_ROW + 2, :, :], zero_b[:, :]).then_inc(q_stacked, 16)
                st, part_of, sem_of = ((q_st[par], q_part, q_stacked), (k_st[par], k_part, k_stacked))[which]
                wait(sp, (high, mid, low)[part][which], b + 1)
                for band, band_part in enumerate((Q_PARTS, K_PARTS)[which]):
                    if band_part == part:
                        sp.dma_start(st[band * HD:(band + 1) * HD, :, :], part_of[:, part, :]).then_inc(sem_of, 16)

            def stack_maxima(b, par, g, step_b, name):
                wait_read(sp, name, step_b)
                first = head_of(g, 0)
                sp.dma_start(q_st[par][MAX_ROW:MAX_ROW + 2, first::SLOTS, :],
                             m_rows[:, :]).then_inc(rows_stacked, 16)

            def store(b):
                wait(sp, o_done, b * NT + NT)
                sp.dma_start(out_d[b], o_sb[:, :, :]).then_inc(stored, 16)

            sp.dma_start(x_in[0][:, :, :], x_d[0]).then_inc(xin_loaded[0], 16)
            sp.dma_start(w_in[:, :], w_attn).then_inc(w_in_loaded, 16)
            sp.dma_start(b_q[:, :], b_attn[0:C].rearrange("(h d a) -> d h a", d=HD, a=1),
                         allow_slow_non_contiguous=True).then_inc(b_qk_loaded, 16)
            sp.dma_start(b_k[:, :], b_attn[C:2 * C].rearrange("(h d a) -> d h a", d=HD, a=1),
                         allow_slow_non_contiguous=True).then_inc(b_qk_loaded, 16)
            for w, wd in enumerate((W_r, W_k, W_v)):
                sp.dma_start(w_ffn[:, w, :], wd).then_inc(w_loaded, 16)
            sp.dma_start(w_o[:, :], w_proj).then_inc(w_loaded, 16)
            sp.dma_start(b_v[:, :], b_attn[2 * C:3 * C].rearrange("(p a) -> p a", a=1)).then_inc(vecs_loaded, 16)
            sp.dma_start(b_o[:, :], b_proj.partition_broadcast(P)).then_inc(vecs_loaded, 16)
            for i, m in enumerate((mu_r, mu_k)):
                sp.dma_start(mu[i][:, :], m.rearrange("(p a) -> p a", a=1)).then_inc(vecs_loaded, 16)
            sp.wait_ge(consts_g, 5)
            sp.dma_start(k_st[0][MAX_ROW:MAX_ROW + 2, :, :], neg_one[:, :]).then_inc(ones_stacked[0], 16)
            sp.wait_ge(consts_v, 4)
            for part in range(3):
                for which in range(2):
                    stack(which, part, 0, 0)
            sp.dma_start(x_in[1][:, :, :], x_d[1]).then_inc(xin_loaded[1], 16)
            sp.wait_ge(consts_g, 11)
            sp.dma_start(k_st[1][MAX_ROW:MAX_ROW + 2, :, :], neg_one[:, :]).then_inc(ones_stacked[1], 16)
            sp.wait_ge(consts_v, 8)
            stack_maxima(0, 0, 0, -1, "maxT3")

            def body(b, par):
                for g in range(SLOTS):
                    if g == 0:
                        if not fixed(b) or b >= 2:
                            wait_read(sp, "proj", b - 1)
                        sp.dma_start(x_res[par][:, :, :], x_d[b]).then_inc(xres_loaded[par], 16)
                    if exists(b, g + 1):
                        if g < SLOTS - 1:
                            stack_maxima(b, par, g + 1, b, f"maxT{g}")
                        else:
                            stack_maxima(b + 1, 1 - par, 0, b, f"maxT{g}")
                    if g == 0 and has_next(b):
                        for part in range(2):
                            for which in range(2):
                                stack(which, part, b + 1, 1 - par)
                    elif g == 1 and has_next(b):
                        for which in range(2):
                            stack(which, 2, b + 1, 1 - par)
                    if g == 2 and (not fixed(b) or b >= 2):
                        store(b - 2)
                    if g == 3 and (not fixed(b) or b + 2 < NB):
                        wait_read(sp, "xT", b - 1)
                        sp.dma_start(x_in[par][:, :, :], x_d[b + 2]).then_inc(xin_loaded[par], 16)

            over_sequences(sp, body)
            store(NB - 2)
            for half in range(2):
                tiles = half_tiles(half)
                sp.wait_ge(o_done, (NB - 1) * NT + tiles.stop)
                sp.dma_start(out_d[NB - 1][:, tiles.start:tiles.stop, :], o_sb[:, tiles.start:tiles.stop, :]
                             ).then_inc(stored, 16)
            sp.wait_ge(stored, 16 * (NB + 1))

        @block.tensor
        def _(pe):
            mm = pe.matmul

            def bank(name, b):
                i = SHARED_BANK[name]
                wait(pe, sh_read[i], shared_use(name, b) - 1)
                return sh_ps[i], sh_full[i]

            def transpose4(name, b, src):
                ps, full = bank(name, b)
                for t in range(NT):
                    last = pe.transpose(ps[:, t * P:(t + 1) * P], src(t), ident[:, :])
                last.then_inc(full, 1)

            def product4(name, b, lhs, rhs):
                ps, full = bank(name, b)
                for t in range(NT):
                    last = mm(ps[:, t * P:(t + 1) * P], lhs[:, t * P:(t + 1) * P], rhs, start=True, stop=True)
                last.then_inc(full, 1)

            def product(name, b, lhs, rhs):
                ps, full = bank(name, b)
                mm(ps[:, :], lhs, rhs, start=True, stop=True).then_inc(full, 1)

            def x_transposed(step_b, b, par):
                wait(pe, xin_loaded[par], (b // 2 + 1) * 16 if fixed(b) else (b - par) * 8 + 16)
                transpose4("xT", step_b, lambda t: x_in[par][:, t, :])

            def queries(step_b):
                wait_read(pe, "xT", step_b)
                product("q", step_b, w_q[:, :], xT[:, :])

            def keys(step_b):
                product("k", step_b, w_k[:, :], xT[:, :])

            def values(step_b):
                product4("v", step_b, xT, w_in[:, 2 * C:3 * C])

            def maxima(b, par, g, u):
                if g == 0 and u == 0:
                    wait(pe, q_stacked, b * Q_DMAS + Q_DMAS)
                    wait(pe, k_stacked, b * K_DMAS + K_DMAS)
                wait(pe, mx_read, b * (SLOTS * MX_UNITS) + (g * MX_UNITS + u - MX_BANKS + 1))
                ps, at = mx_ps[u % MX_BANKS], 0
                for h, t in MX_FILLS[u]:
                    n, hd = (t + 1) * P, head_of(g, h)
                    last = mm(ps[:, at:at + n], q_st[par][:, hd, t * P:(t + 1) * P], k_st[par][:, hd, 0:n],
                              start=True, stop=True)
                    at += n
                last.then_inc(mx_full, 1)

            def logits(b, par, g, u):
                if u == 0:
                    wait(pe, rows_stacked, b * (SLOTS * 16) + (g * 16 + 16))
                (ps, before), at = ex_bank(b, g, u), 0
                wait(pe, exp_done, b * (SLOTS * EX_UNITS) + (g * EX_UNITS + u - before + 1))
                if ps in mx_ps:
                    wait(pe, mx_read, NB * SLOTS * MX_UNITS)
                for h, t in EX_FILLS[u]:
                    n, hd = T - t * P, head_of(g, h)
                    last = mm(ps[:, at:at + n], k_st[par][:, hd, t * P:(t + 1) * P], q_st[par][:, hd, t * P:T],
                              start=True, stop=True)
                    at += n
                last.then_inc(ex_full, 1)

            def max_transposed(name, step_b, b, g):
                wait(pe, m_parts, b * SLOTS + (g + 1))
                ps, full = bank(name, step_b)
                for t in range(NT):
                    last = mm(ps[0:2 * HG, t * P:(t + 1) * P], m_part[:, t, :, :], ident_b[:, :],
                              start=True, stop=True)
                last.then_inc(full, 1)

            def weighted_values(b, par, g, t):
                wait(pe, causal, b * (SLOTS * 2 * NT) + (g * 2 * NT + NT + t + 1))
                if t == 0 and g % 2 == 0:
                    wait(pe, yT_done, b * PAIRS + g // 2)
                if t == 0 and g == 0:
                    wait_read(pe, "v", b - 1)
                for h in range(HG):
                    last = mm(pv_ps[h * VW:(h + 1) * VW, t * P:T], vals[par][:, t, head_of(g, h), :],
                              probs[g % 2][:, h, PCOL[t]:PCOL[t] + T - t * P],
                              start=(t == 0 and g % 2 == 0), stop=(t == NT - 1 and g % 2 == 1),
                              skip_group_check=True)
                if t == NT - 1:
                    last.then_inc(pv_done, 1)

            def back_to_rows(name, step_b, b, j):
                wait(pe, yT_done, b * PAIRS + (j + 1))
                transpose4(name, step_b, lambda t: yT[:, t * P:(t + 1) * P])

            def attention_transposed(step_b):
                wait_read(pe, "Y1", step_b)
                transpose4("ynT", step_b, lambda t: yn[:, t, :])

            def project(step_b):
                wait_read(pe, "ynT", step_b)
                product4("proj", step_b, ynT, w_o[:, :])

            def x1_transposed(step_b, b):
                wait(pe, x1_done, b * NT + NT)
                transpose4("x1T", step_b, lambda t: x1[:, t, :])

            def ffn_in(step_b, b):
                wait(pe, mixed, b * 2 + 1)
                product("kT", step_b, w_ffnT[:, 1, :], mixT[1][:, :])

            def ffn_gate(step_b, b):
                wait(pe, mixed, b * 2 + 2)
                product4("r", step_b, mixT[0], w_ffnT[:, 0, :])

            def ffn_out(step_b, b):
                wait(pe, kact_done, b + 1)
                product4("kv", step_b, kact, w_ffnT[:, 2, :])

            pe.wait_ge(consts_g, 2)
            x_transposed(-1, 0, 0)
            pe.wait_ge(consts_v, 3)
            queries(-1)
            keys(-1)
            values(-1)
            pe.wait_ge(w_loaded, 64)
            ps, full = bank("wT", -1)
            for w in range(3):
                last = pe.transpose(ps[:, w * P:(w + 1) * P], w_ffn[:, w, :], ident[:, :])
            last.then_inc(full, 1)
            pe.wait_ge(consts_v, 5)
            ps, full = bank("bp", -1)
            mm(ps[:, 0:C], b_v_wide[:, :], w_o[:, :], start=True, stop=True).then_inc(full, 1)
            pe.wait_ge(consts_g, 7)
            pe.wait_ge(ones_stacked[0], 16)
            for u in range(MX_UNITS):
                maxima(0, 0, 0, u)
            for u in range(MX_UNITS):
                maxima(0, 0, 1, u)
                if u == 3:
                    max_transposed("maxT3", -1, 0, 0)
            pe.wait_ge(ones_stacked[1], 16)

            def body(b, par):
                for g in range(SLOTS):
                    for step in range(STEPS):
                        if step in EX_AT:
                            logits(b, par, g, EX_AT[step])
                        if exists(b, g + 2):
                            if g < 2:
                                maxima(b, par, g + 2, step)
                            else:
                                maxima(b + 1, 1 - par, g - 2, step)
                        if step in PV_AT and exists(b, g - 1):
                            if g:
                                weighted_values(b, par, g - 1, PV_AT[step])
                            else:
                                weighted_values(b - 1, 1 - par, SLOTS - 1, PV_AT[step])
                        at = g * STEPS + step
                        if at == PE_AT[f"maxT{g}"] and exists(b, g + 1):
                            max_transposed(f"maxT{g}", b, b, g + 1)
                        if at == PE_AT["Y0"]:
                            back_to_rows("Y0", b, b, 0)
                        if has_next(b):
                            if at == PE_AT["xT"]:
                                x_transposed(b, b + 1, 1 - par)
                            if at == PE_AT["q"]:
                                queries(b)
                            if at == PE_AT["k"]:
                                keys(b)
                            if at == PE_AT["v"]:
                                values(b)
                        if has_prev(b):
                            if at == PE_AT["Y1"]:
                                back_to_rows("Y1", b, b - 1, 1)
                            if at == PE_AT["ynT"]:
                                attention_transposed(b)
                            if at == PE_AT["proj"]:
                                project(b)
                            if at == PE_AT["x1T"]:
                                x1_transposed(b, b - 1)
                            if at == PE_AT["kT"]:
                                ffn_in(b, b - 1)
                            if at == PE_AT["r"]:
                                ffn_gate(b, b - 1)
                            if at == PE_AT["kv"]:
                                ffn_out(b, b - 1)

            over_sequences(pe, body)

            last_b = NB - 1
            for t in range(NT):
                weighted_values(last_b, last_b % 2, SLOTS - 1, t)
            back_to_rows("Y1", NB, last_b, 1)
            for half in range(2):
                pe.wait_ge(yn_half, half + 1)
                for t in half_tiles(half):
                    last = pe.transpose(ynT_ps[half][:, in_bank(t)], yn[:, t, :], ident[:, :])
                last.then_inc(ynT_half, 1)
            for half in range(2):
                pe.wait_ge(ynT_copied, half + 1)
                for t in half_tiles(half):
                    last = mm(proj_ps[half][:, in_bank(t)], ynT[:, t * P:(t + 1) * P], w_o[:, :], start=True, stop=True)
                last.then_inc(proj_half, 1)
            for half in range(2):
                pe.wait_ge(x1_done, last_b * NT + half_tiles(half).stop)
                for t in half_tiles(half):
                    last = pe.transpose(x1T_ps[half][:, in_bank(t)], x1[:, t, :], ident[:, :])
                last.then_inc(x1T_half, 1)
            for half in range(2):
                cols = half_cols(half)
                pe.wait_ge(mixed_half, 2 * half + 1)
                mm(kT_ps[half][:, 0:HALF], w_ffnT[:, 1, :], mixT[1][:, cols], start=True, stop=True
                   ).then_inc(kT_half, 1)
                pe.wait_ge(mixed_half, 2 * half + 2)
                for t in half_tiles(half):
                    last = mm(r_ps[half][:, in_bank(t)], mixT[0][:, t * P:(t + 1) * P], w_ffnT[:, 0, :],
                              start=True, stop=True)
                last.then_inc(r_half, 1)
            for half in range(2):
                pe.wait_ge(kact_half, half + 1)
                for t in half_tiles(half):
                    last = mm(kv_ps[half][:, in_bank(t)], kact[:, t * P:(t + 1) * P], w_ffnT[:, 2, :],
                              start=True, stop=True)
                last.then_inc(kv_half, 1)

        @block.scalar
        def _(act):
            def copy(name, b, dst, cols=T):
                ps, read = wait_full(act, name, b)
                act.activation(dst, ps[0:dst.shape[0], 0:cols], ACT.Copy).then_inc(read, 1)

            def exps(b, g, u):
                if u == 0:
                    wait(act, pv_done, b * SLOTS + (g - 1))
                wait(act, ex_full, b * (SLOTS * EX_UNITS) + (g * EX_UNITS + u + 1))
                src = ex_bank(b, g, u)[0][:, :]
                (h, t), *more = EX_FILLS[u]
                if (h + 1, t) in more:
                    src = src.rearrange("p (h q) -> p h q", h=2)
                    dst = probs[g % 2][:, h:h + 2, PCOL[t]:PCOL[t] + T - t * P]
                else:
                    dst = probs[g % 2][:, h, PCOL[t]:PCOL[t] + T]
                act.activation(dst, src, ACT.Exp, scale=SCALE).then_inc(exp_done, 1)

            def max_rows(name, step_b, n):
                wait(act, rows_stacked, n * 16)
                copy(name, step_b, m_rows[:, :])

            def sums(b, j):
                wait(act, pv_done, b * SLOTS + (2 * j + 2))
                if j == 1:
                    wait_full(act, "Y0", b)
                elif has_prev(b):
                    wait_full(act, "Y1", b)
                act.activation(yT[:, :], pv_ps[:, :], ACT.Copy).then_inc(yT_done, 1)

            q_and_k = (("q", q_part, q_rest, b_q), ("k", k_part, k_rest, b_k))

            def highs(i, step_b, b):
                name, part, _, bias = q_and_k[i]
                wait(act, (q_stacked, k_stacked)[i], b * (Q_DMAS, K_DMAS)[i])
                ps, _ = wait_full(act, name, step_b)
                act.activation(part[:, 0, :], ps[:, :], ACT.Identity, bias=bias[:, 0:1]).then_inc(high[i], 1)

            def mids(i, step_b, b):
                name, part, rest, _ = q_and_k[i]
                wait_read(act, name, step_b)
                act.activation(part[:, 1, :], rest[:, :], ACT.Copy).then_inc(mid[i], 1)

            def values(step_b, b, par):
                wait(act, pv_done, b * SLOTS - SLOTS)
                ps, read = wait_full(act, "v", step_b)
                dst = vals[par][:, :, :, :].rearrange("p t (i s) w -> p (t i) s w", s=2)
                src = ps[:, :].rearrange("p (i s d) -> p i s d", s=2, d=HD)
                for s in range(2):
                    last = act.activation(dst[:, :, s, s * HD:(s + 1) * HD], src[:, :, s, :], ACT.Copy)
                last.then_inc(read, 1)

            def share(i, step_b, b):
                wait(act, mixed, b * 2)
                ps, read = wait_full(act, "x1T", step_b)
                m = 1 - i // 2
                if i % 2 == 0:
                    act.activation(mix_cur[m][:, :], ps[:, :], ACT.Copy, scale=mu[m][:, 0:1])
                else:
                    act.activation(mix_prev[m][:, 1:T], ps[:, 0:T - 1], ACT.Copy, scale=mu_rest[m][:, 0:1]
                                   ).then_inc(key_shares if i == 1 else read, 1)

            def ffn_normed(b, tiles):
                wait(act, stored, b * 16)
                wait(act, shift_ready, b + 1)
                for t in tiles:
                    act.activation(o_sb[:, t, :], h2[:, t, :], ACT.Identity, scale=rstd[1][:, t:t + 1],
                                   bias=shift[:, t:t + 1]).then_inc(o_done, 1)

            def rectify(step_b):
                ps, read = wait_full(act, "kT", step_b)
                act.activation(relu[:, :], ps[:, :], ACT.Relu).then_inc(read, 1)

            def gates(step_b):
                ps, read = wait_full(act, "r", step_b)
                act.activation(gate[:, :, :], ps[:, :].rearrange("p (t c) -> p t c", t=NT), ACT.Tanh, scale=0.5
                               ).then_inc(read, 1)

            copy("xT", -1, xT[:, :])
            act.wait_ge(b_qk_loaded, 32)
            highs(0, -1, 0)
            highs(1, -1, 0)
            mids(0, -1, 0)
            mids(1, -1, 0)
            act.wait_ge(consts_g, 10)
            values(-1, 0, 0)
            copy("wT", -1, w_ffnT[:, :, :].rearrange("p w c -> p (w c)"), 3 * C)
            max_rows("maxT3", -1, 0)
            act.wait_ge(consts_g, 14)
            act.wait_ge(consts_v, 7)

            def body(b, par):
                for g in range(SLOTS):
                    for step in range(STEPS):
                        if step in EX_AT:
                            exps(b, g, EX_AT[step])
                        at = g * STEPS + step
                        if at == ACT_AT[f"maxT{g}"] and exists(b, g + 1):
                            max_rows(f"maxT{g}", b, b * SLOTS + (g + 1))
                        if not fixed(b) or b >= 2:
                            if at == ACT_AT["norm2"]:
                                ffn_normed(b - 2, (0, 1))
                            if at == ACT_AT["norm2b"]:
                                ffn_normed(b - 2, (2, 3))
                        if at == ACT_AT["sums0"]:
                            sums(b, 0)
                        if at == ACT_AT["sums1"] and has_prev(b):
                            sums(b - 1, 1)
                        if has_next(b):
                            if at == ACT_AT["xT"]:
                                copy("xT", b, xT[:, :])
                            for i, name in enumerate(("q", "k")):
                                if at == ACT_AT[name]:
                                    highs(i, b, b + 1)
                                if at == ACT_AT[f"{name}_mid"]:
                                    mids(i, b, b + 1)
                            if at == ACT_AT["v"]:
                                values(b, b + 1, 1 - par)
                        if has_prev(b):
                            if at == ACT_AT["ynT"]:
                                copy("ynT", b, ynT[:, :])
                            for i in range(4):
                                if at == ACT_AT[f"share{i}"]:
                                    share(i, b, b - 1)
                            if at == ACT_AT["kT"]:
                                rectify(b)
                            if at == ACT_AT["r"]:
                                gates(b)

            over_sequences(act, body)

            last_b = NB - 1
            sums(last_b, 1)
            ffn_normed(last_b - 1, range(NT))
            for half in range(2):
                cols = half_cols(half)
                act.wait_ge(ynT_half, half + 1)
                act.activation(ynT[:, cols], ynT_ps[half][:, 0:HALF], ACT.Copy).then_inc(ynT_copied, 1)
            for half in range(2):
                first, n = (1, HALF) if half == 0 else (HALF + 1, HALF - 1)
                act.wait_ge(x1T_half, half + 1)
                for i in (1, 0):
                    act.activation(mix_prev[i][:, first:first + n], x1T_ps[half][:, 0:n], ACT.Copy,
                                   scale=mu_rest[i][:, 0:1]).then_inc(prev_half, 1)
            for half in range(2):
                tiles, cols = half_tiles(half), half_cols(half)
                act.wait_ge(kT_half, half + 1)
                act.activation(relu[:, cols], kT_ps[half][:, 0:HALF], ACT.Relu).then_inc(relu_half, 1)
                act.wait_ge(r_half, half + 1)
                act.activation(gate[:, tiles.start:tiles.stop, :],
                               r_ps[half][:, 0:HALF].rearrange("p (t c) -> p t c", c=C), ACT.Tanh, scale=0.5
                               ).then_inc(gate_half, 1)

        @block.vector
        def _(dve):
            def reduce_maxima(b, g, u):
                wait_apart(dve, mx_full, b * (SLOTS * MX_UNITS) + (g * MX_UNITS + u + 1), passed_v)
                at = 0
                for h, t in MX_FILLS[u]:
                    n = (t + 1) * P
                    last = dve.tensor_tensor_reduce(
                        out=masked[u % len(MX_PAIR)][:, at:at + n], in0=mx_ps[u % MX_BANKS][:, at:at + n],
                        in1=mask_wide[:, T - n:T], op0=ALU.add, op1=ALU.max, scale=1.0, scalar=LOWEST,
                        accum_out=m_max[g % 2][:, t, h:h + 1])
                    at += n
                last.then_inc(mx_read, 1)

            def max_parts(b, g, before, before_b):
                s, m = b * SLOTS + g, m_max[g % 2]
                wait(dve, mx_read, b * (SLOTS * MX_UNITS) + (g + 1) * MX_UNITS)
                if before:
                    wait_full(dve, before, before_b)
                dve.tensor_copy(m_part[:, :, 0, :], m[:, :, :]).then_inc(m_hi, 1)
                wait(dve, m_hi, s + 1)
                dve.tensor_tensor(m_part[:, :, 1, :], m[:, :, :], m_part[:, :, 0, :], ALU.subtract).then_inc(m_parts, 1)

            def rests(i, step_b, b):
                name, part, rest, bias = (("q", q_part, q_rest, b_q), ("k", k_part, k_rest, b_k))[i]
                wait(dve, high[i], b + 1)
                wait(dve, low[i], b)
                ps, read = wait_full(dve, name, step_b)
                dve.scalar_tensor_tensor(out=rest[:, :], in0=ps[:, :], scalar=bias[:, 0:1], in1=part[:, 0, :],
                                         op0=ALU.add, op1=ALU.subtract).then_inc(read, 1)

            def normalise(name, step_b, b, j):
                ps, read = wait_full(dve, name, step_b)
                y = ps[:, :].rearrange("p (t h w) -> p (t h) w", t=NT, h=HG)
                r = rden[:, :, :, :].rearrange("p t h s -> p (t h) s")
                dve.reciprocal(r, y[:, :, 2 * HD:2 * HD + 2]).then_inc(rden_done, 1)
                wait(dve, rden_done, b * PAIRS + (j + 1))
                if j == 0 and has_prev(b):
                    wait_full(dve, "ynT", step_b)
                dst = yn[:, :, :].rearrange("p t (h g d) -> p (t h) g d", h=HG, d=HD)[:, :, 2 * j:2 * j + 2, :]
                dve.tensor_tensor(dst, y[:, :, 0:2 * HD].rearrange("p i (s d) -> p i s d", s=2),
                                  r.unsqueeze(3).to_broadcast([P, NT * HG, 2, HD]), ALU.mult).then_inc(read, 1)

            def statistics(i, b, src, tiles):
                for t in tiles:
                    dve.bn_stats(stats[i][:, t, :], src[:, t, :]).then_inc(bn[i], 1)

            def aggregates(i, b):
                wait(dve, rstd_ready[i], b)
                wait_apart(dve, bn[i], b * NT + NT, passed_v)
                for t in range(NT):
                    dve.bn_aggr(mv[i][:, t, :], stats[i][:, t, :]).then_inc(mean_var[i], 1)

            def normed(i, b, src, dst, done, tiles):
                wait(dve, rstd_ready[i], b + 1)
                for t in tiles:
                    dve.tensor_scalar(dst[:, t, :], src[:, t, :], mv[i][:, t, 0:1], rstd[i][:, t:t + 1],
                                      ALU.subtract, ALU.mult).then_inc(done, 1)

            def attention_added(step_b, b, par):
                wait(dve, xres_ready, b + 1)
                wait(dve, x1_done, b * NT)
                ps, read = wait_full(dve, "proj", step_b)
                dve.tensor_tensor(h1[:, :, :], ps[:, :].rearrange("p (t c) -> p t c", t=NT), x_res[par][:, :, :],
                                  ALU.add).then_inc(read, 1)

            def attention_statistics(step_b, b, tiles=range(NT)):
                wait_read(dve, "proj", step_b)
                statistics(0, b, h1, tiles)

            def attention_aggregates(b):
                aggregates(0, b)

            def attention_normed(step_b, b, tiles=range(NT)):
                wait(dve, h2_done, b)
                normed(0, b, h1, x1, x1_done, tiles)

            def ffn_gated(step_b, b):
                wait(dve, o_done, b * NT)
                ps, read = wait_full(dve, "kv", step_b)
                wait_read(dve, "r", step_b)
                dve.scalar_tensor_tensor(out=gated[:, :, :], in0=gate[:, :, :], scalar=1.0,
                                         in1=ps[:, :].rearrange("p (t c) -> p t c", t=NT),
                                         op0=ALU.add, op1=ALU.mult).then_inc(read, 1)

            def ffn_added(step_b, b):
                wait_read(dve, "kv", step_b)
                dve.scalar_tensor_tensor(out=h2[:, :, :], in0=gated[:, :, :], scalar=0.5, in1=x1[:, :, :],
                                         op0=ALU.mult, op1=ALU.add).then_inc(h2_done, 1)

            def ffn_statistics(b, tiles=range(NT)):
                wait(dve, h2_done, b + 1)
                statistics(1, b, h2, tiles)

            def ffn_aggregates(b):
                aggregates(1, b)

            dve.memset(q_st[0][:, 0:NH // 2, :].bitcast(U32), 0).then_inc(consts_v, 1)
            dve.wait_ge(w_in_loaded, 16)
            for i, w in enumerate((w_q, w_k)):
                dve.tensor_copy(w[:, :].rearrange("p (d h) -> p d h", d=HD),
                                w_in[:, i * C:(i + 1) * C].rearrange("p (h d) -> p d h", d=HD)).then_inc(consts_v, 1)
            dve.memset(q_st[0][:, NH // 2:NH, :].bitcast(U32), 0).then_inc(consts_v, 1)
            dve.wait_ge(vecs_loaded, 64)
            dve.tensor_copy(b_v_wide[:, :], b_v[:, 0:1].to_broadcast([P, P])).then_inc(consts_v, 1)
            for i in range(2):
                dve.tensor_scalar(mu_rest[i][:, :], mu[i][:, :], -1.0, 1.0, ALU.mult, ALU.add).then_inc(consts_v, 1)
            dve.wait_ge(b_qk_loaded, 32)
            rests(0, -1, 0)
            rests(1, -1, 0)
            for i, (part, rest) in enumerate(((q_part, q_rest), (k_part, k_rest))):
                dve.wait_ge(mid[i], 1)
                dve.tensor_tensor(part[:, 2, :], rest[:, :], part[:, 1, :], ALU.subtract).then_inc(low[i], 1)
            dve.memset(q_st[1][:, :, :].bitcast(U32), 0).then_inc(consts_v, 1)
            ps, read = wait_full(dve, "bp", -1)
            dve.tensor_tensor(b_out[:, :], ps[:, 0:C], b_o[:, :], ALU.add).then_inc(read, 1)
            dve.wait_ge(mask_ready, 2)
            for g in range(2):
                for u in range(MX_UNITS):
                    reduce_maxima(0, g, u)
                max_parts(0, g, "maxT3" if g else None, -1)

            def body(b, par):
                for g in range(SLOTS):
                    for step in range(STEPS):
                        if exists(b, g + 2):
                            if g < 2:
                                reduce_maxima(b, g + 2, step)
                            else:
                                reduce_maxima(b + 1, g - 2, step)
                        at = g * STEPS + step
                        if at == DVE_AT["Y0"]:
                            normalise("Y0", b, b, 0)
                        if has_next(b):
                            for i, name in enumerate(("q", "k")):
                                if at == DVE_AT[name]:
                                    rests(i, b, b + 1)
                        if not fixed(b) or b >= 2:
                            if at == DVE_AT["aggregates2"]:
                                ffn_aggregates(b - 2)
                        if has_prev(b):
                            if at == DVE_AT["Y1"]:
                                normalise("Y1", b, b - 1, 1)
                            if at == DVE_AT["add1"]:
                                attention_added(b, b - 1, 1 - par)
                            if at == DVE_AT["stats1"]:
                                attention_statistics(b, b - 1, (0, 1))
                            if at == DVE_AT["stats1b"]:
                                attention_statistics(b, b - 1, (2, 3))
                            if at == DVE_AT["aggregates1"]:
                                attention_aggregates(b - 1)
                            if at == DVE_AT["norm1"]:
                                attention_normed(b, b - 1, (0, 1))
                            if at == DVE_AT["norm1b"]:
                                attention_normed(b, b - 1, (2, 3))
                            if at == DVE_AT["gated"]:
                                ffn_gated(b, b - 1)
                            if at == DVE_AT["add2"]:
                                ffn_added(b, b - 1)
                            if at == DVE_AT["stats2"]:
                                ffn_statistics(b - 1, (0, 1))
                            if at == DVE_AT["stats2b"]:
                                ffn_statistics(b - 1, (2, 3))
                    if exists(b, g + 2):
                        if g < 2:
                            max_parts(b, g + 2, f"maxT{g}", b)
                        else:
                            max_parts(b + 1, g - 2, f"maxT{g}", b)

            over_sequences(dve, body)

            last_b = NB - 1
            ffn_aggregates(last_b - 1)
            y_ps, _ = wait_full(dve, "Y1", NB)
            y = y_ps[:, :].rearrange("p (t h w) -> p (t h) w", t=NT, h=HG)
            rec = rden[:, :, :, :].rearrange("p t h s -> p (t h) s")
            dve.reciprocal(rec, y[:, :, 2 * HD:2 * HD + 2]).then_inc(rden_done, 1)
            dve.wait_ge(rden_done, NB * PAIRS)
            for half in range(2):
                part = slice(half * NT * HG // 2, (half + 1) * NT * HG // 2)
                dst = yn[:, :, :].rearrange("p t (h g d) -> p (t h) g d", h=HG, d=HD)[:, part, SLOTS - 2:SLOTS, :]
                dve.tensor_tensor(dst, y[:, part, 0:2 * HD].rearrange("p i (s d) -> p i s d", s=2),
                                  rec[:, part, :].unsqueeze(3).to_broadcast([P, NT * HG // 2, 2, HD]), ALU.mult
                                  ).then_inc(yn_half, 1)

            def sum_statistics(i, half, total, total_done):
                tiles = half_tiles(half)
                dve.wait_ge(total_done, half + 1)
                for t in tiles:
                    dve.bn_stats(stats[i][:, t, :], total[:, t, :]).then_inc(bn[i], 1)
                dve.wait_ge(bn[i], last_b * NT + tiles.stop)
                for t in tiles:
                    dve.bn_aggr(mv[i][:, t, :], stats[i][:, t, :]).then_inc(mean_var[i], 1)

            def half_normed(i, half, total, dst, done):
                dve.wait_ge(rstd_ready[i], last_b + half + 1)
                for t in half_tiles(half):
                    dve.tensor_scalar(dst[:, t, :], total[:, t, :], mv[i][:, t, 0:1], rstd[i][:, t:t + 1],
                                      ALU.subtract, ALU.mult).then_inc(done, 1)

            dve.wait_ge(xres_ready, NB)
            for half in range(2):
                tiles = half_tiles(half)
                dve.wait_ge(proj_half, half + 1)
                dve.tensor_tensor(h1[:, tiles.start:tiles.stop, :],
                                  proj_ps[half][:, 0:HALF].rearrange("p (t c) -> p t c", c=C),
                                  x_res[last_b % 2][:, tiles.start:tiles.stop, :], ALU.add).then_inc(h1_half, 1)
                sum_statistics(0, half, h1, h1_half)
            for half in range(2):
                half_normed(0, half, h1, x1, x1_done)
            for half in range(2):
                dve.wait_ge(prev_half, 2 * half + 2)
                cols = half_cols(half)
                for i in (1, 0):
                    dve.scalar_tensor_tensor(out=mixT[i][:, cols], in0=x1T_ps[half][:, 0:HALF], scalar=mu[i][:, 0:1],
                                             in1=mix_prev[i][:, cols], op0=ALU.mult, op1=ALU.add
                                             ).then_inc(mixed_half, 1)
            for half in range(2):
                cols = half_cols(half)
                dve.wait_ge(relu_half, half + 1)
                dve.tensor_tensor(kact[:, cols], relu[:, cols], relu[:, cols], ALU.mult).then_inc(kact_half, 1)
            for half in range(2):
                tiles = half_tiles(half)
                here = slice(tiles.start, tiles.stop)
                dve.wait_ge(kv_half, half + 1)
                dve.wait_ge(gate_half, half + 1)
                dve.scalar_tensor_tensor(out=gated[:, here, :], in0=gate[:, here, :], scalar=1.0,
                                         in1=kv_ps[half][:, 0:HALF].rearrange("p (t c) -> p t c", c=C),
                                         op0=ALU.add, op1=ALU.mult).then_inc(gated_half, 1)
                dve.wait_ge(gated_half, half + 1)
                dve.scalar_tensor_tensor(out=h2[:, here, :], in0=gated[:, here, :], scalar=0.5, in1=x1[:, here, :],
                                         op0=ALU.mult, op1=ALU.add).then_inc(h2_half, 1)
                sum_statistics(1, half, h2, h2_half)
            dve.wait_ge(stored, 16 * last_b)
            for half in range(2):
                half_normed(1, half, h2, o_sb, o_done)

        @block.gpsimd
        def _(pool):
            def zero_behind(b, g, pair):
                wait_apart(pool, exp_done, b * (SLOTS * EX_UNITS) + (g * EX_UNITS + 5 * pair + 5), passed_g)
                for t in range(NT):
                    blocks = probs[g % 2][:, 2 * pair:2 * pair + 2, PCOL[t]:PCOL[t] + P]
                    pool.affine_select(out=blocks, in_=blocks, compare_op=ALU.is_ge, fill=0.0, base=0,
                                       pattern=[[0, 2], [1, P]], channel_multiplier=-1).then_inc(causal, 1)

            def lows(i, b):
                part, rest = ((q_part, q_rest), (k_part, k_rest))[i]
                wait(pool, mid[i], b + 1)
                pool.tensor_tensor(part[:, 2, :], rest[:, :], part[:, 1, :], ALU.subtract).then_inc(low[i], 1)

            def residual_biased(b, par):
                wait(pool, xres_loaded[par], (b // 2 + 1) * 16 if fixed(b) else (b - par) * 8 + 16)
                pool.tensor_tensor(x_res[par][:, :, :], x_res[par][:, :, :],
                                   b_out[:, :].unsqueeze(1).to_broadcast([P, NT, C]), ALU.add).then_inc(xres_ready, 1)

            def deviations(i, b):
                wait(pool, mean_var[i], b * NT + NT)
                wait_apart(pool, (x1_done, o_done)[i], b * NT, passed_g)
                pool.tensor_scalar(var_eps[i][:, :], mv[i][:, :, 1], EPS, None, ALU.add).then_inc(var_ready[i], 1)
                if i == 1:
                    pool.tensor_scalar(neg_mean[:, :], mv[1][:, :, 0], -1.0, None, ALU.mult).then_inc(neg_mean_ready, 1)
                wait(pool, var_ready[i], b + 1)
                pool.tensor_tensor(rstd[i][:, :], var_eps[i][:, :], exponent[:, :], ALU.pow).then_inc(rstd_ready[i], 1)
                if i == 1:
                    wait(pool, neg_mean_ready, b + 1)
                    wait(pool, rstd_ready[1], b + 1)
                    pool.tensor_tensor(shift[:, :], neg_mean[:, :], rstd[1][:, :], ALU.mult).then_inc(shift_ready, 1)

            def mix(i, step_b, b):
                if i == 1:
                    wait(pool, key_shares, b + 1)
                else:
                    wait_read(pool, "x1T", step_b)
                if has_prev(b):
                    wait_full(pool, ("r", "kT")[i], step_b - 1)
                pool.tensor_tensor(mixT[i][:, :], mix_cur[i][:, :], mix_prev[i][:, :], ALU.add).then_inc(mixed, 1)

            def ones_column(par):
                dst = vals[par][:, :, :, :].rearrange("p t (i s) w -> p (t i) s w", s=2)
                for s in range(2):
                    pool.memset(dst[:, :, s, 2 * HD + s:2 * HD + s + 1], 1.0).then_inc(consts_g, 1)

            def squares(step_b):
                wait_read(pool, "kT", step_b)
                pool.tensor_tensor(kact[:, :], relu[:, :], relu[:, :], ALU.mult).then_inc(kact_done, 1)

            pool.memset(ident[:, :], 0.0).then_inc(consts_g, 1)
            pool.wait_ge(consts_g, 1)
            pool.affine_select(out=ident[:, :], in_=ident[:, :], compare_op=ALU.not_equal, fill=1.0, base=0,
                               pattern=[[-1, P]], channel_multiplier=1).then_inc(consts_g, 1)
            pool.memset(neg_one[:, :], -1.0).then_inc(consts_g, 1)
            pool.memset(zero_b[:, :], 0.0).then_inc(consts_g, 1)
            pool.memset(k_st[0][:, :, :].bitcast(U32), 0).then_inc(consts_g, 1)
            pool.memset(ident_b[:, :], 0.0).then_inc(consts_g, 1)
            pool.wait_ge(consts_g, 6)
            pool.affine_select(out=ident_b[:, :], in_=ident_b[:, :], compare_op=ALU.not_equal, fill=1.0, base=0,
                               pattern=[[-1, P]], channel_multiplier=1).then_inc(consts_g, 1)
            pool.memset(mask_wide[:, :], 0.0).then_inc(mask_ready, 1)
            pool.wait_ge(mask_ready, 1)
            pool.affine_select(out=mask_wide[:, T - P:T], in_=mask_wide[:, T - P:T], compare_op=ALU.is_ge,
                               fill=MASKED, base=0, pattern=[[-1, P]], channel_multiplier=1).then_inc(mask_ready, 1)
            pool.memset(vals[0][:, :, :, :], 0.0).then_inc(consts_g, 1)
            pool.wait_ge(consts_g, 8)
            ones_column(0)
            pool.memset(k_st[1][:, :, :].bitcast(U32), 0).then_inc(consts_g, 1)
            pool.memset(vals[1][:, :, :, :], 0.0).then_inc(consts_g, 1)
            pool.wait_ge(consts_g, 12)
            ones_column(1)
            pool.memset(exponent[:, :], -0.5).then_inc(consts_g, 1)
            for i in range(2):
                pool.memset(mix_prev[i][:, 0:1], 0.0).then_inc(consts_g, 1)
            pool.wait_ge(consts_g, 17)
            wait_read(pool, "bp", -1)

            def others(b, par, at):
                if at == POOL_AT["deviations2"] and (not fixed(b) or b >= 2):
                    deviations(1, b - 2)
                if at == POOL_AT["residual"]:
                    residual_biased(b, par)
                if has_next(b):
                    if at == POOL_AT["q_low"]:
                        lows(0, b + 1)
                    if at == POOL_AT["k_low"]:
                        lows(1, b + 1)
                if has_prev(b):
                    if at == POOL_AT["deviations1"]:
                        deviations(0, b - 1)
                    if at == POOL_AT["mix1"]:
                        mix(1, b, b - 1)
                    if at == POOL_AT["mix0"]:
                        mix(0, b, b - 1)
                    if at == POOL_AT["squares"]:
                        squares(b)

            def body(b, par):
                for g in range(SLOTS):
                    others(b, par, 3 * g)
                    zero_behind(b, g, 0)
                    others(b, par, 3 * g + 1)
                    zero_behind(b, g, 1)
                    others(b, par, 3 * g + 2)

            over_sequences(pool, body)

            last_b = NB - 1
            deviations(1, last_b - 1)
            for i in range(2):
                for half in range(2):
                    tiles = half_tiles(half)
                    here = slice(tiles.start, tiles.stop)
                    pool.wait_ge(mean_var[i], last_b * NT + tiles.stop)
                    pool.tensor_scalar(var_eps[i][:, here], mv[i][:, here, 1], EPS, None, ALU.add
                                       ).then_inc(var_ready[i], 1)
                    pool.wait_ge(var_ready[i], last_b + half + 1)
                    pool.tensor_tensor(rstd[i][:, here], var_eps[i][:, here], exponent[:, here], ALU.pow
                                       ).then_inc(rstd_ready[i], 1)


_INS = ["L0_attn_x", "L0_attn_w_attn", "L0_attn_b_attn", "L0_attn_w_proj", "L0_attn_b_proj",
        "L0_ffn_W_r", "L0_ffn_W_k", "L0_ffn_W_v", "L0_ffn_mu_r", "L0_ffn_mu_k"]


def kernel(**inputs):
    import numpy as _np
    import concourse.bacc as _bacc
    from concourse import mybir as _mybir
    from concourse.bass_utils import run_bass_kernel_spmd as _run

    nc = _bacc.Bacc("TRN2", target_bir_lowering=False, num_devices=1)
    arrays, args = {}, []
    for name in _INS:
        a = _np.ascontiguousarray(inputs[name])
        arrays[f"in_{name}_dram"] = a
        args.append(nc.dram_tensor(f"in_{name}_dram", a.shape, _mybir.dt.from_np(a.dtype), kind="ExternalInput").ap())
    shape = inputs["L0_attn_x"].shape
    args.append(nc.dram_tensor("out_0_dram", shape, _mybir.dt.float32, kind="ExternalOutput").ap())
    block_kernel(nc, *args)
    r = _run(nc, [arrays], core_ids=[0])
    return r.results[0]["out_0_dram"]
```
